# Optimizing a Trainium2 kernel written in Bass

```python
import numpy as np
import jax
import jax.numpy as jnp

def _softmax(x, axis=-1):
    return jax.nn.softmax(x, axis=axis)

def _gelu(x):
    return jax.nn.gelu(x, approximate=True)

def _silu(x):
    return jax.nn.silu(x)

def _sigmoid(x):
    return jax.nn.sigmoid(x)

def _layernorm(x, axis=-1, eps=1e-05):
    m = jnp.mean(x, axis=axis, keepdims=True)
    v = jnp.var(x, axis=axis, keepdims=True)
    return (x - m) / jnp.sqrt(v + eps)

def _scatter_add(tgt, idx, src, axis=0):
    return tgt.at[idx].add(src)

def _segment_sum(src, seg, n):
    return jax.ops.segment_sum(src, seg, n)
kernel_name = 'mk_adaln_d1_jaxref_r8_660649'

def setup_inputs(seed: int=0):
    np.random.seed(seed)
    _w = jnp.asarray

    def _L0_attn_setup():
        import jax, jax.numpy as jnp
        import numpy as np
        B, L, C = (4, 128, 128)
        H = 8
        D = C // H
        MAX_SAMPLES = 32
        HALF_S = MAX_SAMPLES // 2
        S = 2 * HALF_S + 1
        K = 64
        MAX_FREQ = 16.0
        MIN_FREQ = 1.0

        def _silu(v):
            return v * jax.nn.sigmoid(v)
        key = jax.random.key(seed)
        ks = jax.random.split(key, 6)
        x = jax.random.normal(ks[0], (B, L, C), dtype=jnp.float32)
        wave_w = jax.random.normal(ks[1], (2 * H, C), dtype=jnp.float32) * 0.02
        wave_b = jnp.zeros((2 * H,), dtype=jnp.float32)
        kernel_w = jax.random.normal(ks[2], (H * K, C), dtype=jnp.float32) * (0.1 / np.sqrt(C))
        kernel_b = jnp.zeros((H * K,), dtype=jnp.float32)
        out_w = jax.random.normal(ks[3], (C, C), dtype=jnp.float32) * (0.1 / np.sqrt(C))
        return {'x': x, 'wave_w': wave_w, 'wave_b': wave_b, 'kernel_w': kernel_w, 'kernel_b': kernel_b, 'out_w': out_w}
    _L0_attn_in = _L0_attn_setup()

    def _L0_ffn_setup():
        import jax, jax.numpy as jnp
        import numpy as np
        TOP_K = 2
        key = jax.random.key(seed)
        ks = jax.random.split(key, 5)
        B, S, H, E = (2, 128, 128, 8)
        return {'hidden_states': jax.random.normal(ks[0], (B, S, H), dtype=jnp.float32), 'router_w': jax.random.normal(ks[1], (E, H), dtype=jnp.float32) * 0.02, 'router_b': jax.random.normal(ks[2], (E,), dtype=jnp.float32) * 0.02, 'expert_w': jax.random.normal(ks[3], (E, H, H), dtype=jnp.float32) * 0.02, 'expert_b': jax.random.normal(ks[4], (E, H), dtype=jnp.float32) * 0.02}
    _L0_ffn_in = _L0_ffn_setup()
    _L0_c = _w((lambda *s: np.random.randn(*s).astype(np.float32) * 0.05)(16, 128))
    _L0_wmod = _w((lambda *s: np.random.randn(*s).astype(np.float32) * 0.05)(128, 6 * 128) * 128 ** (-0.5))
    _d = {'L0_attn_x': _L0_attn_in['x'], 'L0_attn_wave_w': _L0_attn_in['wave_w'], 'L0_attn_wave_b': _L0_attn_in['wave_b'], 'L0_attn_kernel_w': _L0_attn_in['kernel_w'], 'L0_attn_kernel_b': _L0_attn_in['kernel_b'], 'L0_attn_out_w': _L0_attn_in['out_w'], 'L0_ffn_router_w': _L0_ffn_in['router_w'], 'L0_ffn_router_b': _L0_ffn_in['router_b'], 'L0_ffn_expert_w': _L0_ffn_in['expert_w'], 'L0_ffn_expert_b': _L0_ffn_in['expert_b'], 'L0_c': _L0_c, 'L0_wmod': _L0_wmod}
    _x0 = _d['L0_attn_x']
    _d['L0_attn_x'] = jax.random.normal(jax.random.fold_in(jax.random.key(seed), 1), (16, 256, 128), dtype=_x0.dtype)
    del _x0
    return _d

def reference(L0_attn_x, L0_attn_wave_w, L0_attn_wave_b, L0_attn_kernel_w, L0_attn_kernel_b, L0_attn_out_w, L0_ffn_router_w, L0_ffn_router_b, L0_ffn_expert_w, L0_ffn_expert_b, L0_c, L0_wmod):

    def _L0_attn_ref(x, wave_w, wave_b, kernel_w, kernel_b, out_w):
        import jax, jax.numpy as jnp
        import numpy as np
        B, L, C = (4, 128, 128)
        H = 8
        D = C // H
        MAX_SAMPLES = 32
        HALF_S = MAX_SAMPLES // 2
        S = 2 * HALF_S + 1
        K = 64
        MAX_FREQ = 16.0
        MIN_FREQ = 1.0

        def _silu(v):
            return v * jax.nn.sigmoid(v)
        Bb, Ll, Cc = x.shape
        wave = _silu(x @ wave_w.T + wave_b).reshape(Bb, Ll, 2, H)
        freq = jax.nn.sigmoid(wave[:, :, 0, :]) * (MAX_FREQ - MIN_FREQ) + MIN_FREQ
        phase = jnp.tanh(wave[:, :, 1, :]) * MAX_FREQ
        freq_avg = freq.mean(axis=-1)
        phase_avg = phase.mean(axis=-1)
        kernel = _silu(x @ kernel_w.T + kernel_b).reshape(Bb, Ll, H, K)
        w = kernel[:, :, :, :S]
        s_idx = jnp.arange(S, dtype=x.dtype) - HALF_S
        base = jnp.arange(Ll, dtype=x.dtype)
        pos = base[None, :, None] + s_idx[None, None, :] * freq_avg[:, :, None] + phase_avg[:, :, None]
        pos = jnp.clip(pos, 0.0, Ll - 1.0)
        lo = jnp.floor(pos).astype(jnp.int32)
        hi = jnp.minimum(lo + 1, Ll - 1)
        frac = pos - lo.astype(x.dtype)
        xh = x.reshape(Bb, Ll, H, D)
        b_ix = jnp.arange(Bb)[:, None, None]
        g_lo = xh[b_ix, lo]
        g_hi = xh[b_ix, hi]
        g = g_lo + frac[..., None, None] * (g_hi - g_lo)
        out_h = jnp.einsum('blshd,blhs->blhd', g, w)
        out = out_h.reshape(Bb, Ll, Cc)
        return _silu(out @ out_w.T)

    def _L0_ffn_ref(hidden_states, router_w, router_b, expert_w, expert_b):
        import jax, jax.numpy as jnp
        import numpy as np
        TOP_K = 2
        logits = jnp.einsum('bsh,eh->bse', hidden_states, router_w) + router_b
        routing_weights = jax.nn.softmax(logits, axis=-1)
        _, top_k_indices = jax.lax.top_k(routing_weights, TOP_K)
        E = router_w.shape[0]
        mask = jax.nn.one_hot(top_k_indices, E, dtype=hidden_states.dtype).sum(axis=-2)
        out = jnp.einsum('bse,ehd,bsd->bsh', mask, expert_w, hidden_states)
        out = out + jnp.einsum('bse,eh->bsh', mask, expert_b)
        return out
    x = L0_attn_x
    mod = (_silu(L0_c) @ L0_wmod).reshape(L0_c.shape[0], 6, 1, -1)
    sa, ca, ga, sb, cb, gb = (mod[:, 0], mod[:, 1], mod[:, 2], mod[:, 3], mod[:, 4], mod[:, 5])
    ga = (2 * (ga >= 0) - 1) * jnp.maximum(jnp.abs(ga), 0.25)
    gb = (2 * (gb >= 0) - 1) * jnp.maximum(jnp.abs(gb), 0.25)
    h = _layernorm(x, axis=-1) * (1 + ca) + sa
    x = x + ga * _L0_attn_ref(h, L0_attn_wave_w, L0_attn_wave_b, L0_attn_kernel_w, L0_attn_kernel_b, L0_attn_out_w)
    h = _layernorm(x, axis=-1) * (1 + cb) + sb
    x = x + gb * _L0_ffn_ref(h, L0_ffn_router_w, L0_ffn_router_b, L0_ffn_expert_w, L0_ffn_expert_b)
    return x

_drawn_inputs = setup_inputs


def setup_inputs(seed=0):
    import zlib

    import numpy as np

    out = dict(_drawn_inputs(seed))
    spreads = {'L0_attn_wave_b': (0.0, 0.8), 'L0_attn_kernel_b': (0.0, 0.8)}
    factors = {'L0_attn_wave_w': 8.0,
     'L0_attn_kernel_w': 8.0,
     'L0_attn_out_w': 8.0,
     'L0_ffn_router_b': 2.758,
     'L0_ffn_expert_b': 8.0}
    for name, (base, spread) in spreads.items():
        noise = np.random.default_rng([zlib.crc32(name.encode()), seed]).standard_normal(out[name].shape)
        drawn = base * np.exp(spread * noise) if base else spread * noise
        out[name] = jnp.asarray(drawn.astype(out[name].dtype))
    for name, factor in factors.items():
        out[name] = (out[name] * factor).astype(out[name].dtype)
    return out
```

```python
from contextlib import ExitStack

import numpy as np

import concourse.bass as bass
from concourse import mybir

ALU = mybir.AluOpType
ACT = mybir.ActivationFunctionType
AX = mybir.AxisListType
F32 = mybir.dt.float32
BF16 = mybir.dt.bfloat16
F16 = mybir.dt.float16

P = 128
B, L, C = 16, 256, 128
LT = L // P
H, D = 8, 16
S, HALF = 33, 16
NK = 3
G = -(-L // NK)
LP = NK * G
Q = NK * S
BLK = 6
NB = -(-L // BLK)
NJ = NB + 2
E = 8
EPS = 1e-5
FREQ_MID, FREQ_T = 8.5, 7.5
PHASE = 16.0
REACH = 3.73
MIDDLE = (L - 1) / 2
ROUND = 12582912.0
CHUNKS = [(0, 18), (18, 35), (35, 52), (52, 69), (69, 86)]


def constants():
    q = np.arange(Q)
    k, s = q // S, q % S - HALF
    g = np.arange(G)
    c = {}
    c["ident"] = np.eye(P, dtype=np.float32)
    ctr = np.repeat((BLK * np.arange(NB) + (BLK - 1) / 2 - MIDDLE) / (2 * REACH), G)
    c["ctr"] = np.broadcast_to(ctr, (Q, NB * G)).astype(np.float16)
    c["kmask"] = (k[:, None] == np.arange(NK)[None, :]).astype(np.float32)
    c["posc"] = (G * k[:, None] + g[None, :] + FREQ_MID * s[:, None]).astype(np.float32)
    st = np.zeros((40, NK, Q), np.float32)
    for kk in range(NK):
        st[0:H, kk, :] = (k == kk) * s * FREQ_T / H
        st[32:40, kk, :] = (k == kk) * PHASE / H
    c["spread"] = st.reshape(40, NK * Q)
    v = np.zeros((40, 2), np.float32)
    v[0:H, 0] = FREQ_T / H
    v[32:40, 1] = PHASE / H
    c["mean"] = v
    c["tscale"] = np.where(np.arange(40) < 32, 0.5, 1.0).astype(np.float32)[:, None]
    e = np.zeros((NJ, L), np.float32)
    e[2 + np.arange(L) // BLK, np.arange(L)] = 1.0
    c["expand"] = e
    c["mrow"] = np.broadcast_to(np.arange(L, dtype=np.float32), (P, L)).copy()
    c["lcol"] = (np.arange(P)[:, None] + P * np.arange(LT)[None, :]).astype(np.float32)
    c["fpc"] = np.broadcast_to(np.array([FREQ_MID, 0.0] * LT, np.float32), (P, 2 * LT)).copy()
    c["erow"] = np.broadcast_to(np.arange(E, dtype=np.float32), (P, E)).copy()
    esel = np.zeros((E, E, P), np.float32)
    esel[np.arange(E), np.arange(E), :] = 1.0
    c["esel"] = esel.reshape(E, E * P)
    return c


def build(nc, t):
    ctx = ExitStack()
    with ctx:
        def sb(name, shape, dt=F32):
            return ctx.enter_context(nc.sbuf_tensor(name, shape, dt))

        def bank(name):
            return ctx.enter_context(nc.psum_tensor(name, [P, 512], F32))

        def sem(name):
            return ctx.enter_context(nc.semaphore(name))

        ident = sb("ident", [P, P])
        ctr = sb("ctr", [Q, NB * G], F16)
        kmask = sb("kmask", [Q, NK])
        posc = sb("posc", [Q, G])
        spread = sb("spread", [40, NK, Q])
        mean = sb("mean", [40, 2])
        tscale = sb("tscale", [40, 1])
        expand = sb("expand", [NJ, L])
        mrow = sb("mrow", [P, L])
        lcol = sb("lcol", [P, LT])
        fpc = sb("fpc", [P, 2 * LT])
        erow = sb("erow", [P, E])
        esel32 = sb("esel32", [E, E * P])
        esel = sb("esel", [E, E * P], BF16)
        KWW = (2 * NK - 1) * S
        kwz = sb("kwz", [P, H, KWW])
        kb = sb("kb", [Q, H])
        wvT = sb("wvT", [P, 40])
        wvb = sb("wvb", [40, 1])
        owT = sb("owT", [P, P])
        rwT = sb("rwT", [P, E])
        rb = sb("rb", [P, E])
        weT = sb("weT", [P, E, P])
        eb = sb("eb", [E, P])
        cT = sb("cT", [P, B])
        scT = sb("scT", [P, B])
        wmod = sb("wmod", [P, 6 * C])
        mod = sb("mod", [B, 6 * C])
        gsign = sb("gsign", [B, 2, C]); gabs = sb("gabs", [B, 2, C])
        mhalf = sb("mhalf", [P, LT])
        spare = sb("spare", [P, 1])
        xf = [sb(f"xf{i}", [P, LT, C]) for i in range(2)]
        xk = [sb(f"xk{i}", [P, LT, C]) for i in range(2)]
        mf = [sb(f"mf{i}", [P, 2, C]) for i in range(2)]
        mk = [sb(f"mk{i}", [P, 4, C]) for i in range(2)]
        st1 = sb("st1", [P, LT, 6]); mv1 = sb("mv1", [P, LT, 2]); rs1 = sb("rs1", [P, LT]); ve1 = sb("ve1", [P, LT])
        xn1 = sb("xn1", [P, LT, C]); xm1 = sb("xm1", [P, LT, C])
        h = [sb(f"h{i}", [P, LT, C]) for i in range(2)]
        hT = sb("hT", [P, LP])
        wv = sb("wv", [40, L])
        ft = sb("ft", [40, LP])
        pos = sb("pos", [Q, G])
        pos16 = sb("pos16", [Q, G], F16)
        kap = sb("kap", [Q, 2, G])
        dist = sb("dist", [Q, NB, G], mybir.dt.int16)
        sel = [sb(f"sel{i}", [Q, NJ, G]) for i in range(2)]
        w = sb("w", [Q, G, H])
        wm = [sb(f"wm{i}", [Q, G, NK, H]) for i in range(2)]
        fp = sb("fp", [P, LT, 2]); invf = sb("invf", [P, LT]); lp = sb("lp", [P, LT])
        ca_ = sb("ca_", [P, LT, L]); cb_ = sb("cb_", [P, LT, L])
        cc_ = sb("cc_", [P, LT, L])
        cTm = [sb(f"cTm{i}", [P, LT, L]) for i in range(2)]
        hclip = [sb(f"hclip{i}", [NJ, C]) for i in range(2)]
        pick = sb("pick", [NJ, H, LP])
        A = sb("A", [P, LT, H, L])
        ao = sb("ao", [P, LT, C]); aoT = sb("aoT", [P, L])
        y = sb("y", [P, LT, C]); yg = sb("yg", [P, LT, C]); x2 = sb("x2", [P, LT, C])
        st2 = sb("st2", [P, LT, 6]); mv2 = sb("mv2", [P, LT, 2]); rs2 = sb("rs2", [P, LT]); ve2 = sb("ve2", [P, LT])
        xn2 = sb("xn2", [P, LT, C]); xm2 = sb("xm2", [P, LT, C]); h2 = sb("h2", [P, LT, C])
        h2T = sb("h2T", [P, L])
        lg = sb("lg", [P, LT, E])
        top = sb("top", [P, LT, E]); topi = sb("topi", [P, LT, E], mybir.dt.uint32)
        topf = sb("topf", [P, LT, E]); first = sb("first", [P, LT, E]); mask = sb("mask", [P, LT, E])
        mkT = sb("mkT", [E, L]); mkTb = sb("mkTb", [E, L], BF16)
        hm = sb("hm", [P, E, L])
        moe = sb("moe", [P, LT, C])
        ob = [sb(f"ob{i}", [P, LT, C]) for i in range(2)]

        pw = [bank("pw0"), bank("pw1")]
        pp = [bank("pp0"), bank("pp1")]
        pk = bank("pk")
        pz = bank("pz")
        pf = bank("pf")
        pa = bank("pa")

        s_const = sem("s_const")
        s_zero = sem("s_zero")
        s_wts = sem("s_wts")
        s_wmod = sem("s_wmod")
        s_esel = sem("s_esel")
        s_silc = sem("s_silc"); s_modp = sem("s_modp"); s_modc = sem("s_modc"); s_gate = sem("s_gate")
        s_mod = sem("s_mod"); s_modd = sem("s_modd")
        s_xf = [sem(f"s_xf{i}") for i in range(2)]
        s_mf = [sem(f"s_mf{i}") for i in range(2)]
        s_xk = [sem(f"s_xk{i}") for i in range(2)]
        s_mk = [sem(f"s_mk{i}") for i in range(2)]
        s_clip = [sem(f"s_clip{i}") for i in range(2)]
        s_out = [sem(f"s_out{i}") for i in range(2)]
        v_ln1 = sem("v_ln1")
        s_var1 = sem("s_var1"); s_rstd1 = sem("s_rstd1")
        s_var2 = sem("s_var2"); s_rstd2 = sem("s_rstd2")
        s_h = sem("s_h")
        s_hTp = sem("s_hTp"); s_hT = sem("s_hT")
        s_wvp = sem("s_wvp"); a_wv = sem("a_wv"); s_ft = sem("s_ft")
        s_posp = sem("s_posp")
        s_pos = sem("s_pos"); v_c = sem("v_c"); s_cpre = sem("s_cpre")
        s_fpr = sem("s_fpr")
        a_c = sem("a_c"); s_c = sem("s_c"); s_cTp = sem("s_cTp"); s_cT = sem("s_cT")
        v_sel = sem("v_sel"); s_sel = sem("s_sel")
        s_zp = sem("s_zp"); s_w = sem("s_w"); s_wm = sem("s_wm")
        s_pp = sem("s_pp"); s_pick = sem("s_pick")
        s_pw = sem("s_pw"); s_A = sem("s_A"); s_attn = sem("s_attn")
        s_ao = sem("s_ao"); s_aoTp = sem("s_aoTp"); s_aoT = sem("s_aoT")
        s_yp = sem("s_yp"); s_y = sem("s_y"); v_ln2 = sem("v_ln2"); s_h2 = sem("s_h2")
        s_h2Tp = sem("s_h2Tp"); s_h2T = sem("s_h2T")
        s_lgp = sem("s_lgp"); s_lg = sem("s_lg"); v_top = sem("v_top"); s_mask = sem("s_mask")
        s_mTp = sem("s_mTp"); s_mT = sem("s_mT"); s_mb = sem("s_mb"); s_hm = sem("s_hm")
        s_moe = sem("s_moe"); v_out = sem("v_out"); s_ob = sem("s_ob")

        block = ctx.enter_context(nc.Block())

        class Steps:
            def __init__(self, eng, semaphore, per, b):
                self.eng, self.sem, self.per, self.b, self.k = eng, semaphore, per, b, 0

            def did(self, ins):
                ins.then_inc(self.sem, 1)
                self.k += 1
                assert self.k <= self.per

            def wait(self):
                self.eng.wait_ge(self.sem, self.b * self.per + self.k)

        def hold():
            nc.vector.memset(spare[:, :], 0.0)

        LN1_STEPS, LN2_STEPS, C_STEPS, SEL_STEPS, TOP_STEPS = 4, 6, 7, 5, 4

        def schedule(eng, iteration, prologue=None):
            if prologue:
                prologue()
            iteration(-1, 0, True, False, False)
            iteration(0, 0, True, True, False)
            iteration(1, 0, True, True, True)
            iteration(2, 1, True, True, True)
            with eng.Fori(1, (B - 2) // 2) as r:
                iteration(2 * r + 1, r, True, True, True, 1)
                iteration(2 * r + 2, r + 1, True, True, True, 0)
            iteration(B - 1, (B - 2) // 2, False, True, True)
            iteration(B, B // 2, False, False, True)

        N_CONST = 19
        N_WTS = 1 + NK + 2 + 2

        @block.sync
        def _(sp):
            for dst, name in ((cT[:, :], "cT"), (wmod[:, :], "wmod")):
                sp.dma_start(dst, t[name]).then_inc(s_wmod, 16)
            n = 0
            for dst, name in ((ident[:, :], "ident"), (ctr[:, :], "ctr"), (kmask[:, :], "kmask"), (posc[:, :], "posc"),
                              (spread[:, :, :].rearrange("p a b -> p (a b)"), "spread"), (mean[:, :], "mean"),
                              (tscale[:, :], "tscale"), (expand[:, :], "expand"), (mrow[:, :], "mrow"),
                              (lcol[:, :], "lcol"), (fpc[:, :], "fpc"), (erow[:, :], "erow"), (esel32[:, :], "esel"),
                              (owT[:, :], "owT"), (rwT[:, :], "rwT"), (weT[:, :, :], "weT"), (eb[:, :], "eb"),
                              (rb[:, :], "rb")):
                src = t[name]
                if name == "rb":
                    src = src.rearrange("(a e) -> a e", a=1).to_broadcast([P, E])
                sp.dma_start(dst, src).then_inc(s_const, 16)
                n += 1
            assert n == N_CONST - 1

            def load_front(b, hb, par):
                sp.dma_start(xf[par][:, :, :], t["x"][bass.ds(b, 1)].rearrange("a (t p) c -> p (a t) c", p=P)).then_inc(s_xf[par], 16)
                sp.dma_start(mf[par][:, :, :], t["mod"][bass.ds(b, 1), 0:2].to_broadcast([P, 2, C])).then_inc(s_mf[par], 16)

            def load_back(b, hb, par):
                sp.dma_start(xk[par][:, :, :], t["x"][bass.ds(b, 1)].rearrange("a (t p) c -> p (a t) c", p=P)).then_inc(s_xk[par], 16)
                sp.dma_start(mk[par][:, :, :], t["mod"][bass.ds(b, 1), 2:6].to_broadcast([P, 4, C])).then_inc(s_mk[par], 16)

            sp.wait_ge(s_zero, 4)
            sp.dma_start(kwz[:, :, (NK - 1) * S:NK * S], t["kwT"]).then_inc(s_wts, 16)
            for k in range(NK):
                sp.dma_start(kb[k * S:(k + 1) * S, :], t["kb"]).then_inc(s_wts, 16)
            sp.dma_start(wvT[:, 0:H], t["wvT"][:, 0:H]).then_inc(s_wts, 16)
            sp.dma_start(wvT[:, 32:40], t["wvT"][:, H:2 * H]).then_inc(s_wts, 16)
            sp.dma_start(wvb[0:H, :], t["wvb"][0:H, :]).then_inc(s_wts, 16)
            sp.dma_start(wvb[32:40, :], t["wvb"][H:2 * H, :]).then_inc(s_wts, 16)
            sp.wait_ge(s_mod, 3)
            sp.dma_start(t["mod"].rearrange("b s c -> b (s c)"), mod[:, :]).then_inc(s_modd, 16)
            sp.wait_ge(s_modd, 16)

            def iteration(i, hb, front, mid, back, par=None):
                if par is None:
                    par = i % 2
                if back:
                    sp.wait_ge(s_ob, i)
                else:
                    sp.wait_ge(s_h, i + 2)
                if front:
                    for row, (r_, t_) in enumerate(((0, 0), (P - 1, LT - 1))):
                        sp.dma_start(hclip[1 - par][row:row + 1, :], h[1 - par][r_:r_ + 1, t_, :]).then_inc(s_clip[1 - par], 16)
                if back:
                    sp.dma_start(t["out"][bass.ds(i - 1, 1)].rearrange("a (t p) c -> p (a t) c", p=P),
                                 ob[1 - par][:, :, :]).then_inc(s_out[1 - par], 16)

            load_front(0, 0, 0)
            load_front(1, 0, 1)
            load_back(0, 0, 0)
            iteration(-1, 0, True, False, False)
            load_front(2, 1, 0)
            load_back(1, 0, 1)
            iteration(0, 0, True, True, False)
            load_front(3, 1, 1)
            with sp.Fori(0, (B - 4) // 2) as r:
                for i, par in ((2 * r + 1, 1), (2 * r + 2, 0)):
                    iteration(i, 0, True, True, True, par)
                    load_back(i + 1, 0, 1 - par)
                    load_front(i + 3, 0, 1 - par)
            for i in (B - 3, B - 2):
                iteration(i, 0, True, True, True)
                load_back(i + 1, 0, 1 - i % 2)
            iteration(B - 1, 0, False, True, True)
            iteration(B, 0, False, False, True)
            for p_ in range(2):
                sp.wait_ge(s_out[p_], 16 * B // 2)

        @block.gpsimd
        def _(pool):
            nc.gpsimd.memset(kwz[:, :, :], 0.0).then_inc(s_zero, 1)
            nc.gpsimd.memset(wvT[:, :], 0.0).then_inc(s_zero, 1)
            nc.gpsimd.memset(wvb[:, :], 0.0).then_inc(s_zero, 1)
            nc.gpsimd.memset(hT[:, L:LP], 0.0).then_inc(s_zero, 1)
            nc.gpsimd.memset(ft[:, L:LP], 0.0).then_inc(s_zero, 1)
            nc.gpsimd.memset(hclip[0][:, :], 0.0).then_inc(s_zero, 1)
            nc.gpsimd.memset(hclip[1][:, :], 0.0).then_inc(s_zero, 1)
            nc.gpsimd.memset(mhalf[:, :], -0.5).then_inc(s_zero, 1)
            pool.wait_ge(s_const, 16 * (N_CONST - 1))
            pool.wait_ge(s_zero, 8)
            nc.gpsimd.tensor_copy(esel[:, :], esel32[:, :]).then_inc(s_esel, 1)

            def rstd(b, ready, ve, out, done):
                pool.wait_ge(ready, b + 1)
                nc.gpsimd.tensor_tensor(out[:, :], ve[:, :], mhalf[:, :], ALU.pow).then_inc(done, 1)

            def front_wm(b, par):
                pool.wait_ge(s_w, H * (b + 1))
                if not (isinstance(b, int) and b < 2):
                    pool.wait_ge(s_pp, 5 * (b - 1))
                nc.gpsimd.tensor_tensor(
                    wm[par][:, :, :, :],
                    w[:, :, :].rearrange("p g (a h) -> p g a h", a=1).to_broadcast([Q, G, NK, H]),
                    kmask[:, :].rearrange("p (a k c) -> p a k c", a=1, c=1).to_broadcast([Q, G, NK, H]),
                    ALU.mult).then_inc(s_wm, 1)

            def iteration(i, hb, front, mid, back, par=None):
                if par is None:
                    par = i % 2
                if front:
                    rstd(i + 1, s_var1, ve1, rs1, s_rstd1)
                if back:
                    rstd(i - 1, s_var2, ve2, rs2, s_rstd2)
                if front:
                    front_wm(i + 1, 1 - par)

            schedule(pool, iteration)

        @block.scalar
        def _(act):
            def prologue():
                act.wait_ge(s_wmod, 32)
                nc.scalar.activation(scT[:, :], cT[:, :], ACT.Silu).then_inc(s_silc, 1)
                act.wait_ge(s_modp, 1)
                nc.scalar.activation(mod[:, 0:512], pw[0][0:B, :], ACT.Copy).then_inc(s_modc, 1)
                nc.scalar.activation(mod[:, 512:768], pw[1][0:B, 0:256], ACT.Copy).then_inc(s_modc, 1)
                act.wait_ge(s_const, 16 * (N_CONST - 1))
                act.wait_ge(s_wts, 16 * N_WTS)

            def back_ao(b):
                act.wait_ge(s_attn, b + 1)
                nc.scalar.activation(ao[:, :, :].rearrange("p t c -> p (t c)"), pa[:, 0:L], ACT.Copy).then_inc(s_ao, 1)

            def mid_pick(b, n):
                g0, g1 = CHUNKS[n]
                act.wait_ge(s_pp, 5 * b + n + 1)
                src = pp[n % 2][0:NJ, 0:(g1 - g0) * NK * H].rearrange("p (g k h) -> p g k h", k=NK, h=H)
                dst = pick[:, :, :].rearrange("p h (k g) -> p g k h", g=G)[:, g0:g1]
                nc.scalar.activation(dst, src, ACT.Copy).then_inc(s_pick, 1)

            def back_aoT(b):
                act.wait_ge(s_aoTp, b + 1)
                nc.scalar.activation(aoT[:, :], pk[:, 0:L], ACT.Copy).then_inc(s_aoT, 1)

            def back_y(b):
                act.wait_ge(s_yp, b + 1)
                nc.scalar.activation(y[:, :, :].rearrange("p t c -> p (t c)"), pk[:, L:2 * L], ACT.Silu).then_inc(s_y, 1)

            def front_hT(b):
                act.wait_ge(s_hTp, b + 1)
                nc.scalar.activation(hT[:, 0:L], pf[:, 0:L], ACT.Copy).then_inc(s_hT, 1)

            def front_wave(b):
                act.wait_ge(s_wvp, b + 1)
                nc.scalar.activation(wv[:, :], pf[0:40, L:2 * L], ACT.Silu, bias=wvb[:, 0:1]).then_inc(a_wv, 1)
                act.wait_ge(a_wv, b + 1)
                nc.scalar.activation(ft[:, 0:L], wv[:, :], ACT.Tanh, scale=tscale[:, 0:1]).then_inc(s_ft, 1)

            def back_h2T(b):
                act.wait_ge(s_h2Tp, b + 1)
                nc.scalar.activation(h2T[:, :], pk[:, 0:L], ACT.Copy).then_inc(s_h2T, 1)

            def front_w(b, half):
                act.wait_ge(s_zp, 2 * b + half + 1)
                if half == 0 and not (isinstance(b, int) and b == 0):
                    act.wait_ge(s_wm, b)
                for j in range(4):
                    hh = 4 * half + j
                    nc.scalar.activation(w[:, :, hh], pz[0:Q, j * G:(j + 1) * G], ACT.Silu,
                                         bias=kb[:, hh:hh + 1]).then_inc(s_w, 1)

            def front_c(b):
                act.wait_ge(s_cpre, b + 1)
                nc.scalar.activation(cc_[:, :, :], cb_[:, :, :], ACT.Abs).then_inc(a_c, 1)
                act.wait_ge(a_c, b + 1)
                nc.scalar.activation(cc_[:, :, :], cc_[:, :, :], ACT.Relu, bias=1.0, scale=-1.0).then_inc(s_c, 1)

            def front_cT(b, par):
                act.wait_ge(s_cTp, b + 1)
                nc.scalar.activation(cTm[par][:, :, :].rearrange("p t l -> p (t l)"), pf[:, :], ACT.Copy).then_inc(s_cT, 1)

            def back_mT(b):
                act.wait_ge(s_mTp, b + 1)
                nc.scalar.activation(mkT[:, :], pk[0:E, 0:L], ACT.Copy).then_inc(s_mT, 1)
                nc.scalar.activation(mkTb[:, :], pk[0:E, 0:L], ACT.Copy).then_inc(s_mT, 1)

            def iteration(i, hb, front, mid, back, par=None):
                if par is None:
                    par = i % 2
                if back:
                    back_ao(i - 1)
                if mid:
                    mid_pick(i, 0)
                if back:
                    back_aoT(i - 1)
                if mid:
                    mid_pick(i, 1)
                if back:
                    back_y(i - 1)
                if front:
                    front_hT(i + 1)
                if mid:
                    mid_pick(i, 2)
                if front:
                    front_wave(i + 1)
                if mid:
                    mid_pick(i, 3)
                if back:
                    back_h2T(i - 1)
                if mid:
                    mid_pick(i, 4)
                if front:
                    front_w(i + 1, 0)
                    front_w(i + 1, 1)
                    front_c(i + 1)
                if back:
                    back_mT(i - 1)
                if front:
                    front_cT(i + 1, 1 - par)

            schedule(act, iteration, prologue)

        @block.vector
        def _(dve):
            def prologue():
                dve.wait_ge(s_modc, 2)
                m6 = mod[:, :].rearrange("p (s c) -> p s c", c=C)
                gates = m6[:, 2:6:3, :]
                scales = m6[:, 1:5:3, :]
                nc.vector.tensor_scalar(gsign[:, :, :], gates, 0.0, 2.0, ALU.is_ge, ALU.mult).then_inc(s_gate, 1)
                nc.vector.tensor_scalar(scales, scales, 1.0, None, ALU.add).then_inc(s_mod, 1)
                dve.wait_ge(s_gate, 1)
                nc.vector.scalar_tensor_tensor(gabs[:, :, :], gates, -1.0, gates, ALU.mult, ALU.max).then_inc(s_gate, 1)
                dve.wait_ge(s_gate, 2)
                nc.vector.tensor_scalar(gabs[:, :, :], gabs[:, :, :], 0.25, None, ALU.max).then_inc(s_mod, 1)
                dve.wait_ge(s_mod, 2)
                nc.vector.scalar_tensor_tensor(gates, gsign[:, :, :], -1.0, gabs[:, :, :], ALU.add, ALU.mult).then_inc(s_mod, 1)
                dve.wait_ge(s_const, 16 * (N_CONST - 1))

            def norm(b, st, var_ready, rstd_ready, ve, x_, stats, mv, rstd, xn, xm, scale, shift, out, done):
                for i in range(LT):
                    ins = nc.vector.bn_stats(stats[:, i, :], x_[:, i, :])
                st.did(ins)
                st.wait()
                hold()
                for i in range(LT):
                    ins = nc.vector.bn_aggr(mv[:, i, :], stats[:, i, :])
                st.did(ins)
                st.wait()
                nc.vector.tensor_scalar(ve[:, :], mv[:, :, 1], EPS, None, ALU.add).then_inc(var_ready, 1)
                dve.wait_ge(rstd_ready, b + 1)
                for i in range(LT):
                    ins = nc.vector.tensor_scalar(xn[:, i, :], x_[:, i, :], mv[:, i, 0:1], rstd[:, i:i + 1],
                                                  ALU.subtract, ALU.mult)
                st.did(ins)
                st.wait()
                st.did(nc.vector.tensor_tensor(xm[:, :, :], xn[:, :, :], scale, ALU.mult))
                st.wait()
                nc.vector.tensor_tensor(out, xm[:, :, :], shift, ALU.add).then_inc(done, 1)

            def front_norm(b, hb, par):
                dve.wait_ge(s_xf[par], 16 * (hb + 1))
                dve.wait_ge(s_mf[par], 16 * (hb + 1))
                if not (isinstance(b, int) and b < 2):
                    dve.wait_ge(s_attn, b - 1)
                    dve.wait_ge(s_clip[par], 32 * hb)
                row = lambda j: mf[par][:, j:j + 1, :].to_broadcast([P, LT, C])
                norm(b, Steps(dve, v_ln1, LN1_STEPS, b), s_var1, s_rstd1, ve1, xf[par], st1, mv1, rs1, xn1, xm1, row(1), row(0),
                     h[par][:, :, :], s_h)

            def front_pos(b):
                dve.wait_ge(s_posp, 2 * b + 2)
                nc.vector.tensor_tensor(pos[:, :], pf[0:Q, 0:G], posc[:, :], ALU.add).then_inc(s_pos, 1)
                nc.vector.tensor_tensor(fp[:, :, :].rearrange("p t a -> p (t a)"), pf[:, 128:128 + 2 * LT], fpc[:, :],
                                        ALU.add).then_inc(s_fpr, 1)
                dve.wait_ge(s_fpr, b + 1)
                st = Steps(dve, v_c, C_STEPS, b)
                st.did(nc.vector.reciprocal(invf[:, :], fp[:, :, 0]))
                st.did(nc.vector.tensor_tensor(lp[:, :], lcol[:, :], fp[:, :, 1], ALU.add))
                st.wait()
                if not (isinstance(b, int) and b == 0):
                    dve.wait_ge(s_c, b)
                for i in range(LT):
                    ins = nc.vector.tensor_scalar(ca_[:, i, :], mrow[:, :], lp[:, i:i + 1], invf[:, i:i + 1],
                                                  ALU.subtract, ALU.mult)
                st.did(ins)
                st.wait()
                st.did(nc.vector.tensor_scalar(cb_[:, :, :], ca_[:, :, :], -float(HALF), float(HALF), ALU.max, ALU.min))
                st.wait()
                st.did(nc.vector.tensor_scalar(ca_[:, :, :], cb_[:, :, :], ROUND, ROUND, ALU.add, ALU.subtract))
                st.wait()
                for i in range(LT):
                    ins = nc.vector.tensor_scalar(cb_[:, i, :], ca_[:, i, :], fp[:, i, 0:1], lcol[:, i:i + 1],
                                                  ALU.mult, ALU.add)
                st.did(ins)
                st.wait()
                for i in range(LT):
                    ins = nc.vector.scalar_tensor_tensor(cb_[:, i, :], cb_[:, i, :], fp[:, i, 1:2], mrow[:, :],
                                                         ALU.add, ALU.subtract)
                    if i < LT - 1:
                        st.did(ins)
                ins.then_inc(s_cpre, 1)

            def front_sel(b, par):
                dve.wait_ge(s_pos, b + 1)
                if not (isinstance(b, int) and b < 2):
                    dve.wait_ge(s_pp, 5 * (b - 1))
                st = Steps(dve, v_sel, SEL_STEPS, b)
                st.did(nc.vector.tensor_scalar(kap[:, 0, :], pos[:, :], -1.0, 0.0, ALU.mult, ALU.max))
                st.did(nc.vector.tensor_scalar(kap[:, 1, :], pos[:, :], -float(L - 1), 0.0, ALU.add, ALU.max))
                st.did(nc.vector.tensor_scalar(pos16[:, :], pos[:, :], MIDDLE, 0.5 / REACH, ALU.subtract, ALU.mult))
                st.wait()
                st.did(nc.vector.tensor_scalar(sel[par][:, 0:2, :], kap[:, :, :], 1.0, None, ALU.min))
                st.did(nc.vector.tensor_tensor(
                    dist[:, :, :], pos16[:, :].rearrange("p (a g) -> p a g", a=1).to_broadcast([Q, NB, G]),
                    ctr[:, :].rearrange("p (j g) -> p j g", g=G), ALU.subtract))
                st.wait()
                nc.vector.tensor_scalar(sel[par][:, 2:NJ, :], dist[:, :, :], 0.0, None, ALU.is_equal).then_inc(s_sel, 1)

            def mid_A(b, hp, par):
                if hp == 0:
                    dve.wait_ge(s_cT, b + 1)
                for m in range(LT):
                    dve.wait_ge(s_pw, 8 * b + 2 * hp + m + 1)
                    nc.vector.tensor_tensor(
                        A[:, m, 2 * hp:2 * hp + 2, :], pw[m][:, :].rearrange("p (h l) -> p h l", h=2),
                        cTm[par][:, m:m + 1, :].to_broadcast([P, 2, L]), ALU.mult).then_inc(s_A, 1)

            def back_norm(b, hb, par):
                dve.wait_ge(s_xk[par], 16 * (hb + 1))
                dve.wait_ge(s_mk[par], 16 * (hb + 1))
                dve.wait_ge(s_y, b + 1)
                row = lambda j: mk[par][:, j:j + 1, :].to_broadcast([P, LT, C])
                st = Steps(dve, v_ln2, LN2_STEPS, b)
                st.did(nc.vector.tensor_tensor(yg[:, :, :], y[:, :, :], row(0), ALU.mult))
                st.wait()
                st.did(nc.vector.tensor_tensor(x2[:, :, :], yg[:, :, :], xk[par][:, :, :], ALU.add))
                st.wait()
                norm(b, st, s_var2, s_rstd2, ve2, x2, st2, mv2, rs2, xn2, xm2, row(2), row(1), h2[:, :, :], s_h2)

            def back_logits(b):
                dve.wait_ge(s_lgp, b + 1)
                nc.vector.tensor_tensor(
                    lg[:, :, :], pk[:, L:L + LT * E].rearrange("p (t e) -> p t e", e=E),
                    rb[:, :].rearrange("p (a e) -> p a e", a=1).to_broadcast([P, LT, E]), ALU.add).then_inc(s_lg, 1)

            def back_top(b):
                dve.wait_ge(s_lg, b + 1)
                hold()
                st = Steps(dve, v_top, TOP_STEPS, b)
                for i in range(LT):
                    ins = nc.vector.max(top[:, i, :], lg[:, i, :])
                st.did(ins)
                st.wait()
                hold()
                for i in range(LT):
                    ins = nc.vector.max_index(topi[:, i, :], top[:, i, :], lg[:, i, :])
                st.did(ins)
                st.wait()
                st.did(nc.vector.tensor_copy(topf[:, :, :], topi[:, :, :]))
                st.wait()
                for i in range(LT):
                    ins = nc.vector.tensor_scalar(first[:, i, :], erow[:, :], topf[:, i, 0:1], None, ALU.is_equal)
                st.did(ins)
                st.wait()
                if not (isinstance(b, int) and b == 0):
                    dve.wait_ge(s_mTp, b)
                for i in range(LT):
                    ins = nc.vector.scalar_tensor_tensor(mask[:, i, :], erow[:, :], topf[:, i, 1:2], first[:, i, :],
                                                         ALU.is_equal, ALU.add)
                ins.then_inc(s_mask, 1)

            def back_hm(b, n):
                dve.wait_ge(s_mb, 4 * b + n + 1)
                nc.vector.tensor_tensor(
                    hm[:, 2 * n:2 * n + 2, :], pk[:, :].rearrange("p (e l) -> p e l", e=2),
                    h2T[:, :].rearrange("p (a l) -> p a l", a=1).to_broadcast([P, 2, L]), ALU.mult).then_inc(s_hm, 1)

            def back_out(b, hb, par):
                dve.wait_ge(s_moe, b + 1)
                if not (isinstance(b, int) and b < 2):
                    dve.wait_ge(s_out[par], 16 * hb)
                nc.vector.tensor_tensor(moe[:, :, :], pz[:, 0:L].rearrange("p (t c) -> p t c", c=C),
                                        mk[par][:, 3:4, :].to_broadcast([P, LT, C]), ALU.mult).then_inc(v_out, 1)
                dve.wait_ge(v_out, b + 1)
                nc.vector.tensor_tensor(ob[par][:, :, :], moe[:, :, :], x2[:, :, :], ALU.add).then_inc(s_ob, 1)

            def iteration(i, hb, front, mid, back, par=None):
                if par is None:
                    par = i % 2
                fh = (i + 1) // 2 if isinstance(i, int) else (hb if par == 0 else hb + 1)
                bh = (i - 1) // 2 if isinstance(i, int) else (hb - 1 if par == 0 else hb)
                if front:
                    front_norm(i + 1, fh, 1 - par)
                if back:
                    back_norm(i - 1, bh, 1 - par)
                if front:
                    front_pos(i + 1)
                if back:
                    back_logits(i - 1)
                    back_top(i - 1)
                if front:
                    front_sel(i + 1, 1 - par)
                if mid:
                    mid_A(i, 0, par)
                    mid_A(i, 1, par)
                if back:
                    back_hm(i - 1, 0)
                    back_hm(i - 1, 1)
                if mid:
                    mid_A(i, 2, par)
                if back:
                    back_hm(i - 1, 2)
                if mid:
                    mid_A(i, 3, par)
                if back:
                    back_hm(i - 1, 3)
                    back_out(i - 1, bh, 1 - par)

            schedule(dve, iteration, prologue)

        @block.tensor
        def _(pe):
            mm = nc.tensor.matmul

            def prologue():
                pe.wait_ge(s_silc, 1)
                mm(pw[0][0:B, :], scT[:, :], wmod[:, 0:512], start=True, stop=True)
                mm(pw[1][0:B, 0:256], scT[:, :], wmod[:, 512:768], start=True, stop=True).then_inc(s_modp, 1)
                pe.wait_ge(s_const, 16 * (N_CONST - 1))
                pe.wait_ge(s_wts, 16 * N_WTS)
                pe.wait_ge(s_zero, 7)
                pe.wait_ge(s_esel, 1)
                pe.wait_ge(s_modc, 2)

            def mid_select(b, n, par):
                g0, g1 = CHUNKS[n]
                if n == 0:
                    pe.wait_ge(s_sel, b + 1)
                    pe.wait_ge(s_wm, b + 1)
                if n >= 2:
                    pe.wait_ge(s_pick, 5 * b + n - 1)
                elif not (isinstance(b, int) and b == 0):
                    pe.wait_ge(s_pick, 5 * b)
                for g in range(g0, g1):
                    ins = mm(pp[n % 2][0:NJ, (g - g0) * NK * H:(g - g0 + 1) * NK * H], sel[par][:, :, g],
                             wm[par][:, g, :, :].rearrange("p k h -> p (k h)"), start=True, stop=True)
                ins.then_inc(s_pp, 1)

            def mid_expand(b, hp):
                if hp == 0:
                    pe.wait_ge(s_pick, 5 * b + 5)
                for m in range(LT):
                    n = 2 * hp + m
                    if n >= 2:
                        pe.wait_ge(s_A, 8 * b + n - 1)
                    elif not (isinstance(b, int) and b == 0):
                        pe.wait_ge(s_A, 8 * b + n - 1)
                    mm(pw[m][:, :], expand[:, m * P:(m + 1) * P], pick[:, 2 * hp:2 * hp + 2, 0:L],
                       start=True, stop=True).then_inc(s_pw, 1)

            def mid_attend(b, hp, par, hb):
                if hp == 0:
                    if not (isinstance(b, int) and b == 0):
                        pe.wait_ge(s_ao, b)
                    pe.wait_ge(s_clip[par], 32 * (hb + 1))
                pe.wait_ge(s_A, 8 * b + 2 * hp + 2)
                for i in range(LT):
                    rows = slice(i * P, (i + 1) * P)
                    for hh in (2 * hp, 2 * hp + 1):
                        cols = slice(hh * D, (hh + 1) * D)
                        dst = pa[:, i * C + hh * D:i * C + (hh + 1) * D]
                        for m in range(LT):
                            mm(dst, A[:, m, hh, rows], h[par][:, m, cols], start=(m == 0), stop=False)
                        ins = mm(dst, pick[:, hh, rows], hclip[par][:, cols], start=False, stop=True)
                if hp == 3:
                    ins.then_inc(s_attn, 1)

            def front_hT(b, par):
                pe.wait_ge(s_h, b + 1)
                if not (isinstance(b, int) and b == 0):
                    pe.wait_ge(s_cT, b)
                for i in range(LT):
                    ins = nc.tensor.transpose(pf[:, i * P:(i + 1) * P], h[par][:, i, :], ident[:, :])
                ins.then_inc(s_hTp, 1)

            def front_wave(b):
                pe.wait_ge(s_hT, b + 1)
                mm(pf[0:40, L:2 * L], wvT[:, :], hT[:, 0:L], start=True, stop=True).then_inc(s_wvp, 1)

            def front_pos(b):
                pe.wait_ge(s_ft, b + 1)
                for k in range(NK):
                    ins = mm(pf[0:Q, 0:G], spread[:, k, :], ft[:, k * G:(k + 1) * G], start=(k == 0), stop=(k == NK - 1))
                ins.then_inc(s_posp, 1)
                for i in range(LT):
                    ins = mm(pf[:, 128 + 2 * i:130 + 2 * i], ft[:, i * P:(i + 1) * P], mean[:, :], start=True, stop=True)
                ins.then_inc(s_posp, 1)

            def front_project(b, half):
                if half == 1:
                    pe.wait_ge(s_w, H * b + 4)
                elif not (isinstance(b, int) and b < 3):
                    pe.wait_ge(v_out, b - 2)
                for j in range(4):
                    for k in range(NK):
                        lo = (NK - 1 - k) * S
                        ins = mm(pz[0:Q, j * G:(j + 1) * G], kwz[:, 4 * half + j, lo:lo + Q],
                                 hT[:, k * G:(k + 1) * G], start=(k == 0), stop=(k == NK - 1))
                ins.then_inc(s_zp, 1)

            def front_cT(b):
                pe.wait_ge(s_c, b + 1)
                pe.wait_ge(s_pos, b + 1)
                pe.wait_ge(s_fpr, b + 1)
                for m in range(LT):
                    for i in range(LT):
                        ins = nc.tensor.transpose(pf[:, m * L + i * P:m * L + (i + 1) * P],
                                                  cc_[:, i, m * P:(m + 1) * P], ident[:, :])
                ins.then_inc(s_cTp, 1)

            def back_aoT(b):
                pe.wait_ge(s_ao, b + 1)
                if not (isinstance(b, int) and b == 0):
                    pe.wait_ge(s_hm, 4 * b)
                for i in range(LT):
                    ins = nc.tensor.transpose(pk[:, i * P:(i + 1) * P], ao[:, i, :], ident[:, :])
                ins.then_inc(s_aoTp, 1)

            def back_y(b):
                pe.wait_ge(s_aoT, b + 1)
                for i in range(LT):
                    ins = mm(pk[:, L + i * C:L + (i + 1) * C], aoT[:, i * P:(i + 1) * P], owT[:, :], start=True, stop=True)
                ins.then_inc(s_yp, 1)

            def back_h2T(b):
                pe.wait_ge(s_h2, b + 1)
                for i in range(LT):
                    ins = nc.tensor.transpose(pk[:, i * P:(i + 1) * P], h2[:, i, :], ident[:, :])
                ins.then_inc(s_h2Tp, 1)

            def back_router(b):
                pe.wait_ge(s_h2T, b + 1)
                for i in range(LT):
                    ins = mm(pk[:, L + i * E:L + (i + 1) * E], h2T[:, i * P:(i + 1) * P], rwT[:, :], start=True, stop=True)
                ins.then_inc(s_lgp, 1)

            def back_mT(b):
                pe.wait_ge(s_mask, b + 1)
                for i in range(LT):
                    ins = nc.tensor.transpose(pk[0:E, i * P:(i + 1) * P], mask[:, i, :], ident[:, :])
                ins.then_inc(s_mTp, 1)

            def back_mb(b, n):
                if n == 0:
                    pe.wait_ge(s_mT, 2 * b + 2)
                    pe.wait_ge(s_lg, b + 1)
                else:
                    pe.wait_ge(s_hm, 4 * b + n)
                for j in range(2):
                    e = 2 * n + j
                    ins = mm(pk[:, j * L:(j + 1) * L], esel[:, e * P:(e + 1) * P], mkTb[:, :], start=True, stop=True)
                ins.then_inc(s_mb, 1)

            def back_experts(b, whole=True):
                pe.wait_ge(s_hm, 4 * b + 4)
                for i in range(LT):
                    dst = pz[:, i * C:(i + 1) * C]
                    for e in range(E):
                        mm(dst, hm[:, e, i * P:(i + 1) * P], weT[:, e, :], start=(e == 0), stop=False)
                    ins = mm(dst, mkT[:, i * P:(i + 1) * P], eb[:, :], start=False, stop=True)
                ins.then_inc(s_moe, 1)

            def iteration(i, hb, front, mid, back, par=None):
                if par is None:
                    par = i % 2
                mh = i // 2 if isinstance(i, int) else hb
                F = lambda f, *a: f(*a) if front else None
                M = lambda f, *a: f(*a) if mid else None
                K = lambda f, *a: f(*a) if back else None
                M(mid_select, i, 0, par)
                K(back_aoT, i - 1)
                M(mid_select, i, 1, par)
                K(back_y, i - 1)
                F(front_hT, i + 1, 1 - par)
                M(mid_select, i, 2, par)
                F(front_wave, i + 1)
                M(mid_select, i, 3, par)
                K(back_h2T, i - 1)
                F(front_pos, i + 1)
                M(mid_select, i, 4, par)
                K(back_router, i - 1)
                F(front_project, i + 1, 0)
                M(mid_expand, i, 0)
                F(front_project, i + 1, 1)
                M(mid_expand, i, 1)
                M(mid_attend, i, 0, par, mh)
                K(back_mT, i - 1)
                F(front_cT, i + 1)
                M(mid_expand, i, 2)
                K(back_mb, i - 1, 0)
                M(mid_attend, i, 1, par, mh)
                K(back_mb, i - 1, 1)
                M(mid_expand, i, 3)
                K(back_mb, i - 1, 2)
                M(mid_attend, i, 2, par, mh)
                K(back_mb, i - 1, 3)
                M(mid_attend, i, 3, par, mh)
                K(back_experts, i - 1)

            schedule(pe, iteration, prologue)


def kernel(L0_attn_x, L0_attn_wave_w, L0_attn_wave_b, L0_attn_kernel_w, L0_attn_kernel_b, L0_attn_out_w,
           L0_ffn_router_w, L0_ffn_router_b, L0_ffn_expert_w, L0_ffn_expert_b, L0_c, L0_wmod):
    import concourse.bacc as bacc
    from concourse.bass_utils import run_bass_kernel_spmd

    a = lambda x: np.ascontiguousarray(np.asarray(x))
    K = L0_attn_kernel_w.shape[0] // H
    arrays = constants()
    arrays["x"] = a(L0_attn_x)
    arrays["kwT"] = a(np.asarray(L0_attn_kernel_w).reshape(H, K, C)[:, :S].transpose(2, 0, 1))
    arrays["kb"] = a(np.asarray(L0_attn_kernel_b).reshape(H, K)[:, :S].T)
    arrays["wvT"] = a(np.asarray(L0_attn_wave_w).T)
    arrays["wvb"] = a(np.asarray(L0_attn_wave_b).reshape(2 * H, 1))
    arrays["owT"] = a(np.asarray(L0_attn_out_w).T)
    arrays["rwT"] = a(np.asarray(L0_ffn_router_w).T)
    arrays["rb"] = a(L0_ffn_router_b)
    arrays["weT"] = a(np.asarray(L0_ffn_expert_w).transpose(2, 0, 1))
    arrays["eb"] = a(L0_ffn_expert_b)
    arrays["cT"] = a(np.asarray(L0_c).T)
    arrays["wmod"] = a(L0_wmod)

    nc = bacc.Bacc("TRN2", target_bir_lowering=False, num_devices=1)
    t, feed = {}, {}
    for name, v in arrays.items():
        v = a(v)
        feed[f"in_{name}"] = v
        t[name] = nc.dram_tensor(f"in_{name}", v.shape, mybir.dt.from_np(v.dtype), kind="ExternalInput").ap()
    t["mod"] = nc.dram_tensor("mod_rows", (B, 6, C), F32, kind="Internal").ap()
    t["out"] = nc.dram_tensor("out_0", (B, L, C), F32, kind="ExternalOutput").ap()
    build(nc, t)
    r = run_bass_kernel_spmd(nc, [feed], core_ids=[0])
    return r.results[0]["out_0"]
```

```python
from contextlib import ExitStack

import numpy as np

import concourse.bass as bass
from concourse import mybir

ALU = mybir.AluOpType
ACT = mybir.ActivationFunctionType
AX = mybir.AxisListType
F32 = mybir.dt.float32
BF16 = mybir.dt.bfloat16
F16 = mybir.dt.float16

P = 128
B, L, C = 16, 256, 128
LT = L // P
H, D = 8, 16
S, HALF = 33, 16
NK = 3
G = -(-L // NK)
LP = NK * G
Q = NK * S
BLK = 6
NB = -(-L // BLK)
NP = 3
PH = NP * H
LOW, HIGH = 17, 19
NX = 2 * H
E = 8
EPS = 1e-5
FREQ_MID, FREQ_T = 8.5, 7.5
PHASE = 16.0
REACH = 3.73
MIDDLE = (L - 1) / 2
ROUND = 12582912.0
PER = 512 // (NK * PH)
CHUNKS = [(g, min(g + PER, G)) for g in range(0, G, PER)]
NC = len(CHUNKS)
NW = H * S


def constants():
    q = np.arange(Q)
    k, s = q // S, q % S - HALF
    g = np.arange(G)
    c = {}
    c["ident"] = np.eye(P, dtype=np.float32)
    ctr = np.repeat((BLK * np.arange(NB) + (BLK - 1) / 2 - MIDDLE) / (2 * REACH), G)
    c["ctr"] = np.broadcast_to(ctr, (Q, NB * G)).astype(np.float16)
    c["kmask"] = (k[:, None] == np.arange(NK)[None, :]).astype(np.float32)
    c["posc"] = (G * k[:, None] + g[None, :] + FREQ_MID * s[:, None]).astype(np.float32)
    st = np.zeros((40, NK, Q), np.float32)
    for kk in range(NK):
        st[0:H, kk, :] = (k == kk) * s * FREQ_T / H
        st[32:40, kk, :] = (k == kk) * PHASE / H
    c["spread"] = st.reshape(40, NK * Q)
    v = np.zeros((40, 2), np.float32)
    v[0:H, 0] = FREQ_T / H
    v[32:40, 1] = PHASE / H
    c["mean"] = v
    c["tscale"] = np.where(np.arange(40) < 32, 0.5, 1.0).astype(np.float32)[:, None]
    e = np.zeros((P, L), np.float32)
    e[np.arange(L) // BLK, np.arange(L)] = 1.0
    c["expand"] = e
    c["mrow"] = np.broadcast_to(np.arange(L, dtype=np.float32), (P, L)).copy()
    c["lcol"] = (np.arange(P)[:, None] + P * np.arange(LT)[None, :]).astype(np.float32)
    c["fpc"] = np.broadcast_to(np.array([FREQ_MID, 0.0] * LT, np.float32), (P, 2 * LT)).copy()
    c["erow"] = np.broadcast_to(np.arange(E, dtype=np.float32), (P, E)).copy()
    c["srow"] = np.broadcast_to(np.arange(S, dtype=np.float32) - HALF, (P, S)).copy()
    ends = np.zeros((P, LT, NX), np.float32)
    ends[0, 0, :H] = 1.0
    ends[P - 1, LT - 1, H:] = 1.0
    c["ends"] = ends.reshape(P, LT * NX)
    own = (np.arange(NX)[:, None] % H == np.arange(C)[None, :] // D).astype(np.float32)
    c["own"] = own * np.where(np.arange(NX) < H, -1.0, 1.0).astype(np.float32)[:, None]
    esel = np.zeros((E, E, P), np.float32)
    esel[np.arange(E), np.arange(E), :] = 1.0
    c["esel"] = esel.reshape(E, E * P)
    return c


def build(nc, t):
    ctx = ExitStack()
    with ctx:
        def sb(name, shape, dt=F32):
            return ctx.enter_context(nc.sbuf_tensor(name, shape, dt))

        def bank(name):
            return ctx.enter_context(nc.psum_tensor(name, [P, 512], F32))

        def sem(name):
            return ctx.enter_context(nc.semaphore(name))

        ident = sb("ident", [P, P])
        ctr = sb("ctr", [Q, NB * G], F16)
        kmask = sb("kmask", [Q, NK])
        posc = sb("posc", [Q, G])
        spread = sb("spread", [40, NK, Q])
        mean = sb("mean", [40, 2])
        tscale = sb("tscale", [40, 1])
        expand32 = sb("expand32", [P, L])
        expand = sb("expand", [P, L], BF16)
        srow = sb("srow", [P, S])
        ends = sb("ends", [P, LT, NX])
        own = sb("own", [NX, C])
        kwl = sb("kwl", [P, NW])
        kbl = sb("kbl", [NP, NW]); kbr = sb("kbr", [NP, NW]); kbs = sb("kbs", [NP, NP, NW], BF16)
        kbt = sb("kbt", [NP, 2, NW], BF16); kbp = sb("kbp", [NP, NW], BF16)
        one = sb("one", [NP, P], BF16)
        mrow = sb("mrow", [P, L])
        lcol = sb("lcol", [P, LT])
        fpc = sb("fpc", [P, 2 * LT])
        erow = sb("erow", [P, E])
        esel32 = sb("esel32", [E, E * P])
        esel = sb("esel", [E, E * P], BF16)
        KWW = (2 * NK - 1) * S
        kwz = sb("kwz", [P, H, KWW])
        kb = sb("kb", [Q, H])
        wvT = sb("wvT", [P, 40])
        wvb = sb("wvb", [40, 1])
        owT = sb("owT", [P, P])
        rwT = sb("rwT", [P, E])
        rb = sb("rb", [P, E])
        weT = sb("weT", [P, E, P])
        eb = sb("eb", [E, P])
        cT = sb("cT", [P, B])
        scT = sb("scT", [P, B])
        wmod = sb("wmod", [P, 6 * C])
        mod = sb("mod", [B, 6 * C])
        gsign = sb("gsign", [B, 2, C]); gabs = sb("gabs", [B, 2, C])
        mhalf = sb("mhalf", [P, LT])
        spare = sb("spare", [P, 1]); zero = sb("zero", [P, 1])
        xf = [sb(f"xf{i}", [P, LT, C]) for i in range(2)]
        xk = [sb(f"xk{i}", [P, LT, C]) for i in range(2)]
        mf = [sb(f"mf{i}", [P, 2, C]) for i in range(2)]
        mk = [sb(f"mk{i}", [P, 4, C]) for i in range(2)]
        st1 = sb("st1", [P, LT, 6]); mv1 = sb("mv1", [P, LT, 2]); rs1 = sb("rs1", [P, LT]); ve1 = sb("ve1", [P, LT])
        xn1 = sb("xn1", [P, LT, C]); xm1 = sb("xm1", [P, LT, C])
        hs = [sb(f"hs{i}", [P, LT * H, 2 * D]) for i in range(2)]
        h = sb("h", [P, LT, C]); hT = sb("hT", [P, LP])
        wv = sb("wv", [40, L])
        ft = sb("ft", [40, LP])
        pos = sb("pos", [Q, G])
        pos16 = sb("pos16", [Q, G], F16)
        dist = sb("dist", [Q, NB, G], mybir.dt.int16)
        sel = sb("sel", [Q, NB, G], BF16)
        w = sb("w", [Q, G, H])
        wr = sb("wr", [Q, G, H]); wp = sb("wp", [Q, G, PH], BF16)
        wm = sb("wm", [Q, G, NK * PH], BF16)
        wl = sb("wl", [P, LT, NW]); posl = sb("posl", [P, LT, S])
        kl = sb("kl", [P, LT, LOW]); kh = sb("kh", [P, LT, HIGH])
        pl = sb("pl", [P, LT * H, LOW]); ph = sb("ph", [P, LT * H, HIGH])
        clip = sb("clip", [P, LT, NX])
        clipT = [sb(f"clipT{i}", [P, L]) for i in range(2)]
        fp = sb("fp", [P, LT, 2]); invf = sb("invf", [P, LT]); lp = sb("lp", [P, LT]); nlf = sb("nlf", [P, LT])
        ca_ = sb("ca_", [P, LT, L]); cb_ = sb("cb_", [P, LT, L])
        cc_ = sb("cc_", [P, LT, L])
        cTm = sb("cTm", [P, LT, L])
        hclip = [sb(f"hclip{i}", [P, C]) for i in range(2)]
        pick = sb("pick", [P, PH, LP], BF16)
        A = sb("A", [P, LT, H, L])
        aoT = sb("aoT", [P, L])
        y = sb("y", [P, LT, C]); yg = sb("yg", [P, LT, C]); x2 = [sb(f"x2{i}", [P, LT, C]) for i in range(2)]
        st2 = sb("st2", [P, LT, 6]); mv2 = sb("mv2", [P, LT, 2]); rs2 = sb("rs2", [P, LT]); ve2 = sb("ve2", [P, LT])
        xn2 = sb("xn2", [P, LT, C]); xm2 = sb("xm2", [P, LT, C]); h2 = sb("h2", [P, LT, C])
        h2T = sb("h2T", [P, L])
        lg = sb("lg", [P, LT, E])
        top = sb("top", [P, LT, E]); topi = sb("topi", [P, LT, E], mybir.dt.uint32)
        topf = sb("topf", [P, LT, E]); top1 = sb("top1", [P, LT, E]); mask = sb("mask", [P, LT, E])
        mkT = sb("mkT", [E, L]); mkTb = sb("mkTb", [E, L], BF16)
        hm = sb("hm", [P, E, L])
        moe = sb("moe", [P, LT, C])
        ob = [sb(f"ob{i}", [P, LT, C]) for i in range(2)]

        pw = [bank("pw0"), bank("pw1")]
        pp = [bank("pp0"), bank("pp1")]
        pk = bank("pk")
        pz = bank("pz")
        pf = bank("pf")
        pa = bank("pa")

        s_const = sem("s_const")
        s_zero = sem("s_zero")
        s_wts = sem("s_wts")
        s_wmod = sem("s_wmod")
        s_esel = sem("s_esel")
        s_silc = sem("s_silc"); s_modp = sem("s_modp"); s_modc = sem("s_modc"); s_gate = sem("s_gate")
        s_mod = sem("s_mod"); s_modd = sem("s_modd")
        s_xf = [sem(f"s_xf{i}") for i in range(2)]
        s_mf = [sem(f"s_mf{i}") for i in range(2)]
        s_xk = [sem(f"s_xk{i}") for i in range(2)]
        s_mk = [sem(f"s_mk{i}") for i in range(2)]
        s_out = [sem(f"s_out{i}") for i in range(2)]
        v_cast = sem("v_cast")
        v_ln1 = sem("v_ln1")
        s_var1 = sem("s_var1"); s_rstd1 = sem("s_rstd1")
        s_var2 = sem("s_var2"); s_rstd2 = sem("s_rstd2")
        s_xn1 = sem("s_xn1"); p_xm1 = sem("p_xm1")
        s_h = sem("s_h")
        s_hs = sem("s_hs")
        s_hTp = sem("s_hTp"); s_hT = sem("s_hT")
        s_wvp = sem("s_wvp"); a_wv = sem("a_wv"); s_ft = sem("s_ft")
        s_posp = sem("s_posp")
        s_hc = sem("s_hc")
        s_pos = sem("s_pos")
        s_fpr = sem("s_fpr")
        v_lin = sem("v_lin"); s_lin = sem("s_lin")
        a_ca = sem("a_ca"); v_cl = sem("v_cl"); s_rnd = sem("s_rnd"); a_cb = sem("a_cb"); p_cc = sem("p_cc")
        a_c = sem("a_c"); s_c = sem("s_c"); s_cTp = sem("s_cTp"); s_cT = sem("s_cT")
        v_sel = sem("v_sel"); s_sel = sem("s_sel")
        s_zp = sem("s_zp"); s_w = sem("s_w")
        p_split = sem("p_split")
        s_wm = sem("s_wm")
        s_wlp = sem("s_wlp"); s_wl = sem("s_wl")
        v_kap = sem("v_kap"); s_kap = sem("s_kap"); s_prod = sem("s_prod"); s_clip = sem("s_clip")
        s_clTp = sem("s_clTp"); s_clT = sem("s_clT")
        s_pp = sem("s_pp"); s_pick = sem("s_pick")
        s_pw = sem("s_pw"); s_A = sem("s_A"); s_attn = sem("s_attn")
        s_aoT = sem("s_aoT")
        s_yp = sem("s_yp"); s_y = sem("s_y"); v_x2 = sem("v_x2"); v_ln2 = sem("v_ln2"); v_h2 = sem("v_h2"); s_h2 = sem("s_h2")
        s_h2Tp = sem("s_h2Tp"); s_h2T = sem("s_h2T")
        s_lgp = sem("s_lgp"); s_lg = sem("s_lg"); v_top = sem("v_top"); s_mask = sem("s_mask")
        s_mTp = sem("s_mTp"); s_mT = sem("s_mT"); s_mb = sem("s_mb"); s_hm = sem("s_hm")
        s_moe = sem("s_moe"); v_out = sem("v_out"); s_ob = sem("s_ob")

        block = ctx.enter_context(nc.Block())

        class Steps:
            def __init__(self, eng, semaphore, per, b):
                self.eng, self.sem, self.per, self.b, self.k = eng, semaphore, per, b, 0

            def did(self, ins):
                ins.then_inc(self.sem, 1)
                self.k += 1
                assert self.k <= self.per

            def wait(self):
                self.eng.wait_ge(self.sem, self.b * self.per + self.k)

        def hold():
            nc.vector.memset(spare[:, :], 0.0)

        LN1_STEPS, LN2_STEPS, LIN_STEPS, KAP_STEPS, TOP_STEPS, SPLIT = 2, 2, 2, 3, 4, 4
        MOE_LAG = 2

        def first(b, n=1):
            return isinstance(b, int) and b < n

        def h_of(par):
            return hs[par][:, :, :].rearrange("p (x a) (q d) -> p x (a q) d", a=2, q=2)[:, :, 0:4:3, :]

        def schedule(eng, iteration, i0, r0, r1, i1):
            def steps(i, r):
                def run_buf(lag, stage, *args):
                    n = i + lag
                    if r is not None:
                        stage(2 * r + n, r + n // 2, n % 2, *args)
                    elif 0 <= n < B:
                        stage(n, n // 2, n % 2, *args)

                def run(lag, stage, *args):
                    run_buf(lag, lambda b, half, par: stage(b, *args))
                iteration(run, run_buf)

            for i in range(i0, 2 * r0):
                steps(i, None)
            with eng.Fori(r0, r1) as r:
                steps(0, r)
                steps(1, r)
            for i in range(2 * r1, i1 + 1):
                steps(i, None)

        N_CONST = 24
        N_WTS = 1 + NK + 2 + 2

        @block.sync
        def _(sp):
            for dst, name in ((cT[:, :], "cT"), (wmod[:, :], "wmod")):
                sp.dma_start(dst, t[name]).then_inc(s_wmod, 16)
            n = 0
            for dst, name in ((ident[:, :], "ident"), (ctr[:, :], "ctr"), (kmask[:, :], "kmask"), (posc[:, :], "posc"),
                              (spread[:, :, :].rearrange("p a b -> p (a b)"), "spread"), (mean[:, :], "mean"),
                              (tscale[:, :], "tscale"), (expand32[:, :], "expand"), (srow[:, :], "srow"),
                              (ends[:, :, :].rearrange("p a b -> p (a b)"), "ends"), (own[:, :], "own"),
                              (kwl[:, :].rearrange("p (h s) -> p h s", h=H), "kwT"), (kbl[:, :], "kbl"), (mrow[:, :], "mrow"),
                              (lcol[:, :], "lcol"), (fpc[:, :], "fpc"), (erow[:, :], "erow"), (esel32[:, :], "esel"),
                              (owT[:, :], "owT"), (rwT[:, :], "rwT"), (weT[:, :, :], "weT"), (eb[:, :], "eb"),
                              (rb[:, :], "rb")):
                src = t[name]
                if name == "rb":
                    src = src.rearrange("(a e) -> a e", a=1).to_broadcast([P, E])
                if name == "kbl":
                    src = src.to_broadcast([NP, NW])
                sp.dma_start(dst, src).then_inc(s_const, 16)
                n += 1
            assert n == N_CONST - 1

            def load_front(b, par):
                sp.dma_start(xf[par][:, :, :], t["x"][bass.ds(b, 1)].rearrange("a (t p) c -> p (a t) c", p=P)).then_inc(s_xf[par], 16)
                sp.dma_start(mf[par][:, :, :], t["mod"][bass.ds(b, 1), 0:2].to_broadcast([P, 2, C])).then_inc(s_mf[par], 16)

            def load_back(b, par):
                sp.dma_start(xk[par][:, :, :], t["x"][bass.ds(b, 1)].rearrange("a (t p) c -> p (a t) c", p=P)).then_inc(s_xk[par], 16)
                sp.dma_start(mk[par][:, :, :], t["mod"][bass.ds(b, 1), 2:6].to_broadcast([P, 4, C])).then_inc(s_mk[par], 16)

            sp.wait_ge(s_zero, 4)
            sp.dma_start(kwz[:, :, (NK - 1) * S:NK * S], t["kwT"]).then_inc(s_wts, 16)
            for k in range(NK):
                sp.dma_start(kb[k * S:(k + 1) * S, :], t["kb"]).then_inc(s_wts, 16)
            sp.dma_start(wvT[:, 0:H], t["wvT"][:, 0:H]).then_inc(s_wts, 16)
            sp.dma_start(wvT[:, 32:40], t["wvT"][:, H:2 * H]).then_inc(s_wts, 16)
            sp.dma_start(wvb[0:H, :], t["wvb"][0:H, :]).then_inc(s_wts, 16)
            sp.dma_start(wvb[32:40, :], t["wvb"][H:2 * H, :]).then_inc(s_wts, 16)
            sp.wait_ge(s_mod, 3)
            sp.dma_start(t["mod"].rearrange("b s c -> b (s c)"), mod[:, :]).then_inc(s_modd, 16)
            sp.wait_ge(s_modd, 16)

            def store(b, par):
                sp.wait_ge(s_ob, b + 1)
                sp.dma_start(t["out"][bass.ds(b, 1)].rearrange("a (t p) c -> p (a t) c", p=P),
                             ob[par][:, :, :]).then_inc(s_out[par], 16)

            for b in range(2):
                load_front(b, b)
                load_back(b, b)

            def after_h(b, par):
                sp.wait_ge(s_hs, b + 1)
                load_front(b + 2, par)

            def after_out(b, par):
                store(b, par)
                load_back(b + 2, par)

            AHEAD = 3
            def step(b):
                if b >= AHEAD:
                    (after_out if b - AHEAD + 2 < B else store)(b - AHEAD, (b - AHEAD) % 2)
                if b + 2 < B:
                    after_h(b, b % 2)

            for b in range(AHEAD + 1):
                step(b)
            with sp.Fori(2, (B - 2) // 2) as r:
                for par in range(2):
                    after_out(2 * r + par - AHEAD, 1 - par)
                    after_h(2 * r + par, par)
            for b in range(B - 2, B + AHEAD):
                step(b)
            for p_ in range(2):
                sp.wait_ge(s_out[p_], 16 * B // 2)

        N_ZERO = 13

        @block.gpsimd
        def _(pool):
            nc.gpsimd.memset(kwz[:, :, :], 0.0).then_inc(s_zero, 1)
            nc.gpsimd.memset(wvT[:, :], 0.0).then_inc(s_zero, 1)
            nc.gpsimd.memset(wvb[:, :], 0.0).then_inc(s_zero, 1)
            nc.gpsimd.memset(mhalf[:, :], -0.5).then_inc(s_zero, 1)
            nc.gpsimd.memset(zero[:, :], 0.0).then_inc(s_zero, 1)
            nc.gpsimd.memset(hs[0][:, :, :], 0.0).then_inc(s_zero, 1)
            nc.gpsimd.memset(hs[1][:, :, :], 0.0).then_inc(s_zero, 1)
            nc.gpsimd.memset(hT[:, L:LP], 0.0).then_inc(s_zero, 1)
            nc.gpsimd.memset(ft[:, L:LP], 0.0).then_inc(s_zero, 1)
            nc.gpsimd.memset(hclip[0][:, :], 0.0).then_inc(s_zero, 1)
            nc.gpsimd.memset(hclip[1][:, :], 0.0).then_inc(s_zero, 1)
            nc.gpsimd.memset(clipT[0][:, :], 0.0).then_inc(s_zero, 1)
            nc.gpsimd.memset(clipT[1][:, :], 0.0).then_inc(s_zero, 1)
            pool.wait_ge(s_const, 16 * (N_CONST - 1))
            pool.wait_ge(s_zero, N_ZERO)
            nc.gpsimd.tensor_copy(esel[:, :], esel32[:, :]).then_inc(s_esel, 1)

            def front_rstd(b):
                pool.wait_ge(s_var1, b + 1)
                nc.gpsimd.tensor_tensor(rs1[:, :], ve1[:, :], mhalf[:, :], ALU.pow).then_inc(s_rstd1, 1)

            def back_rstd(b):
                pool.wait_ge(s_var2, b + 1)
                nc.gpsimd.tensor_tensor(rs2[:, :], ve2[:, :], mhalf[:, :], ALU.pow).then_inc(s_rstd2, 1)

            def front_h(b, half, par):
                pool.wait_ge(s_xn1, b + 1)
                nc.gpsimd.tensor_tensor(xm1[:, :, :], xn1[:, :, :], mf[par][:, 1:2, :].to_broadcast([P, LT, C]),
                                        ALU.mult).then_inc(p_xm1, 1)
                pool.wait_ge(p_xm1, b + 1)
                nc.gpsimd.tensor_tensor(h[:, :, :], xm1[:, :, :], mf[par][:, 0:1, :].to_broadcast([P, LT, C]),
                                        ALU.add).then_inc(s_h, 1)

            def front_hs(b, half, par):
                pool.wait_ge(s_h, b + 1)
                if not first(b, 2):
                    pool.wait_ge(s_attn, b - 1)
                for i in range(LT):
                    ins = nc.gpsimd.tensor_tensor(
                        h_of(par)[:, i * H // 2:(i + 1) * H // 2],
                        xm1[:, i, :].rearrange("p (j a d) -> p j a d", a=2, d=D),
                        mf[par][:, 0, :].rearrange("p (j a d) -> p j a d", a=2, d=D), ALU.add)
                ins.then_inc(s_hs, 1)

            def front_dist(b):
                pool.wait_ge(a_cb, b + 1)
                if not first(b):
                    pool.wait_ge(s_cTp, b)
                nc.gpsimd.tensor_tensor(cc_[:, :, :], cb_[:, :, :],
                                        mrow[:, :].rearrange("p (a l) -> p a l", a=1).to_broadcast([P, LT, L]),
                                        ALU.subtract).then_inc(p_cc, 1)

            def front_split(b, step):
                if step == 0:
                    pool.wait_ge(s_w, H * (b + 1))
                    if not first(b):
                        pool.wait_ge(s_wm, b)
                else:
                    pool.wait_ge(p_split, SPLIT * b + step)
                src = w if step < 2 else wr
                here = wp[:, :, step // 2 * H:(step // 2 + 1) * H]
                if step % 2 == 0:
                    nc.gpsimd.tensor_tensor(here, src[:, :, :], zero[0:Q, :].rearrange("p (a b) -> p a b", b=1)
                                            .to_broadcast([Q, G, H]), ALU.add).then_inc(p_split, 1)
                else:
                    rest = wr[:, :, :] if step == 1 else wp[:, :, 2 * H:3 * H]
                    nc.gpsimd.tensor_tensor(rest, src[:, :, :], here, ALU.subtract).then_inc(p_split, 1)

            def front_prod(b):
                pool.wait_ge(s_kap, b + 1)
                pool.wait_ge(s_wl, 2 * b + 2)
                if not first(b):
                    pool.wait_ge(s_clip, b)
                for i in range(LT):
                    wrow = wl[:, i, :].rearrange("p (h s) -> p h s", s=S)
                    nc.gpsimd.tensor_tensor(pl[:, i * H:(i + 1) * H, :], wrow[:, :, 0:LOW],
                                            kl[:, i:i + 1, :].to_broadcast([P, H, LOW]), ALU.mult)
                    ins = nc.gpsimd.tensor_tensor(ph[:, i * H:(i + 1) * H, :], wrow[:, :, S - HIGH:S],
                                                  kh[:, i:i + 1, :].to_broadcast([P, H, HIGH]), ALU.mult)
                ins.then_inc(s_prod, 1)

            def iteration(run, run_buf):
                run(1, front_rstd)
                run(0, front_dist)
                run(0, front_split, 0)
                run(0, front_split, 1)
                run(0, front_split, 2)
                run(0, front_split, 3)
                run_buf(1, front_h)
                run(-1, back_rstd)
                run(0, front_prod)
                run_buf(1, front_hs)

            schedule(pool, iteration, -1, 1, 7, 16)

        @block.scalar
        def _(act):
            def prologue():
                act.wait_ge(s_wmod, 32)
                nc.scalar.activation(scT[:, :], cT[:, :], ACT.Silu).then_inc(s_silc, 1)
                act.wait_ge(s_modp, 1)
                nc.scalar.activation(mod[:, 0:512], pw[0][0:B, :], ACT.Copy).then_inc(s_modc, 1)
                nc.scalar.activation(mod[:, 512:768], pw[1][0:B, 0:256], ACT.Copy).then_inc(s_modc, 1)
                act.wait_ge(s_const, 16 * (N_CONST - 1))
                act.wait_ge(s_wts, 16 * N_WTS)

            def back_aoT(b):
                act.wait_ge(s_attn, b + 1)
                nc.scalar.activation(aoT[:, :], pa[:, 0:L], ACT.Copy).then_inc(s_aoT, 1)

            def mid_pick(b, n):
                g0, g1 = CHUNKS[n]
                act.wait_ge(s_pp, NC * b + n + 1)
                if n == 0 and not first(b):
                    act.wait_ge(s_pw, 8 * b)
                src = pp[n % 2][0:NB, 0:(g1 - g0) * NK * PH].rearrange("p (g k x) -> p g k x", k=NK, x=PH)
                dst = pick[0:NB, :, :].rearrange("p x (k g) -> p g k x", g=G)[:, g0:g1]
                nc.scalar.activation(dst, src, ACT.Copy).then_inc(s_pick, 1)

            def back_y(b):
                act.wait_ge(s_yp, b + 1)
                nc.scalar.activation(y[:, :, :].rearrange("p t c -> p (t c)"), pk[:, L:2 * L], ACT.Silu).then_inc(s_y, 1)

            def front_hT(b):
                act.wait_ge(s_hTp, b + 1)
                if not first(b):
                    act.wait_ge(s_zp, 2 * b)
                    act.wait_ge(s_wlp, 2 * b)
                nc.scalar.activation(hT[:, 0:L], pf[:, 0:L], ACT.Copy).then_inc(s_hT, 1)

            def front_wave(b):
                act.wait_ge(s_wvp, b + 1)
                nc.scalar.activation(wv[:, :], pf[0:40, L:2 * L], ACT.Silu, bias=wvb[:, 0:1]).then_inc(a_wv, 1)
                act.wait_ge(a_wv, b + 1)
                nc.scalar.activation(ft[:, 0:L], wv[:, :], ACT.Tanh, scale=tscale[:, 0:1]).then_inc(s_ft, 1)

            def back_h2T(b):
                act.wait_ge(s_h2Tp, b + 1)
                nc.scalar.activation(h2T[:, :], pk[:, 0:L], ACT.Copy).then_inc(s_h2T, 1)

            def front_w(b, half):
                act.wait_ge(s_zp, 2 * b + half + 1)
                if half == 0 and not first(b):
                    act.wait_ge(p_split, SPLIT * b)
                for j in range(4):
                    hh = 4 * half + j
                    nc.scalar.activation(w[:, :, hh], pz[0:Q, j * G:(j + 1) * G], ACT.Silu,
                                         bias=kb[:, hh:hh + 1]).then_inc(s_w, 1)

            def front_wl(b, i):
                act.wait_ge(s_wlp, 2 * b + i + 1)
                if i == 0 and not first(b):
                    act.wait_ge(s_prod, b)
                nc.scalar.activation(wl[:, i, :], (pf, pa)[i][:, 0:NW], ACT.Silu).then_inc(s_wl, 1)

            def front_number(b):
                act.wait_ge(s_lin, b + 1)
                for i in range(LT):
                    ins = nc.scalar.activation(ca_[:, i, :], mrow[:, :], ACT.Identity, bias=nlf[:, i:i + 1],
                                               scale=invf[:, i:i + 1])
                ins.then_inc(a_ca, 1)

            def front_near(b):
                act.wait_ge(s_rnd, b + 1)
                for i in range(LT):
                    ins = nc.scalar.activation(cb_[:, i, :], ca_[:, i, :], ACT.Identity, bias=lp[:, i:i + 1],
                                               scale=fp[:, i, 0:1])
                ins.then_inc(a_cb, 1)

            def front_c(b):
                act.wait_ge(p_cc, b + 1)
                nc.scalar.activation(cc_[:, :, :], cc_[:, :, :], ACT.Abs).then_inc(a_c, 1)
                act.wait_ge(a_c, b + 1)
                nc.scalar.activation(cc_[:, :, :], cc_[:, :, :], ACT.Relu, bias=1.0, scale=-1.0).then_inc(s_c, 1)

            def front_clT(b, half, par):
                act.wait_ge(s_clTp, b + 1)
                nc.scalar.activation(clipT[par][0:NX, :], pa[0:NX, 0:L], ACT.Copy).then_inc(s_clT, 1)

            def front_cT(b):
                act.wait_ge(s_cTp, b + 1)
                if not first(b):
                    act.wait_ge(s_A, 8 * b)
                nc.scalar.activation(cTm[:, :, :].rearrange("p t l -> p (t l)"), pf[:, :], ACT.Copy).then_inc(s_cT, 1)

            def back_mT(b):
                act.wait_ge(s_mTp, b + 1)
                nc.scalar.activation(mkT[:, :], pk[0:E, 0:L], ACT.Copy).then_inc(s_mT, 1)
                nc.scalar.activation(mkTb[:, :], pk[0:E, 0:L], ACT.Copy).then_inc(s_mT, 1)

            def iteration(run, run_buf):
                run(0, front_c)
                run(0, front_cT)
                run(-1, back_aoT)
                run(-1, back_y)
                run(0, mid_pick, 0)
                run(0, mid_pick, 1)
                run(1, front_hT)
                run(0, mid_pick, 2)
                run(0, mid_pick, 3)
                run(1, front_wave)
                run(0, mid_pick, 4)
                run(0, mid_pick, 5)
                run(0, front_wl, 1)
                run(-1, back_h2T)
                run(0, mid_pick, 6)
                run(0, mid_pick, 7)
                run(1, front_number)
                run(0, mid_pick, 8)
                run(1, front_w, 0)
                run(0, mid_pick, 9)
                run(0, mid_pick, 10)
                run(-1, back_mT)
                run(0, mid_pick, 11)
                run(0, mid_pick, 12)
                run(1, front_near)
                run(1, front_wl, 0)
                run(1, front_w, 1)
                run_buf(0, front_clT)

            prologue()
            schedule(act, iteration, -1, 1, 7, 16)

        @block.vector
        def _(dve):
            def prologue():
                nc.vector.memset(pick[:, :, :], 0.0).then_inc(v_cast, 1)
                nc.vector.memset(one[:, :], 1.0).then_inc(v_cast, 1)
                dve.wait_ge(s_modc, 2)
                m6 = mod[:, :].rearrange("p (s c) -> p s c", c=C)
                gates = m6[:, 2:6:3, :]
                scales = m6[:, 1:5:3, :]
                nc.vector.tensor_scalar(gsign[:, :, :], gates, 0.0, 2.0, ALU.is_ge, ALU.mult).then_inc(s_gate, 1)
                nc.vector.tensor_scalar(scales, scales, 1.0, None, ALU.add).then_inc(s_mod, 1)
                dve.wait_ge(s_gate, 1)
                nc.vector.scalar_tensor_tensor(gabs[:, :, :], gates, -1.0, gates, ALU.mult, ALU.max).then_inc(s_gate, 1)
                dve.wait_ge(s_gate, 2)
                nc.vector.tensor_scalar(gabs[:, :, :], gabs[:, :, :], 0.25, None, ALU.max).then_inc(s_mod, 1)
                dve.wait_ge(s_mod, 2)
                nc.vector.scalar_tensor_tensor(gates, gsign[:, :, :], -1.0, gabs[:, :, :], ALU.add, ALU.mult).then_inc(s_mod, 1)
                dve.wait_ge(s_const, 16 * (N_CONST - 1))
                nc.vector.tensor_copy(expand[:, :], expand32[:, :]).then_inc(v_cast, 1)
                nc.vector.tensor_copy(kbs[:, 0, :], kbl[:, :]).then_inc(v_cast, 1)
                dve.wait_ge(v_cast, 4)
                nc.vector.tensor_tensor(kbr[:, :], kbl[:, :], kbs[:, 0, :], ALU.subtract).then_inc(v_cast, 1)
                dve.wait_ge(v_cast, 5)
                nc.vector.tensor_copy(kbs[:, 1, :], kbr[:, :]).then_inc(v_cast, 1)
                dve.wait_ge(v_cast, 6)
                nc.vector.tensor_tensor(kbs[:, 2, :], kbr[:, :], kbs[:, 1, :], ALU.subtract).then_inc(v_cast, 1)
                nc.vector.tensor_scalar(kbt[:, 0, :], kbs[:, 0, :], ident[0:NP, 0:1], None, ALU.mult).then_inc(v_cast, 1)
                dve.wait_ge(v_cast, 8)
                nc.vector.scalar_tensor_tensor(kbt[:, 1, :], kbs[:, 1, :], ident[0:NP, 1:2], kbt[:, 0, :],
                                               ALU.mult, ALU.add).then_inc(v_cast, 1)
                dve.wait_ge(v_cast, 9)
                nc.vector.scalar_tensor_tensor(kbp[:, :], kbs[:, 2, :], ident[0:NP, 2:3], kbt[:, 1, :],
                                               ALU.mult, ALU.add).then_inc(v_cast, 1)

            def variance(st, x_, stats, mv, ve, ready):
                for i in range(LT):
                    ins = nc.vector.bn_stats(stats[:, i, :], x_[:, i, :])
                st.did(ins)
                st.wait()
                hold()
                for i in range(LT):
                    ins = nc.vector.bn_aggr(mv[:, i, :], stats[:, i, :])
                st.did(ins)
                st.wait()
                nc.vector.tensor_scalar(ve[:, :], mv[:, :, 1], EPS, None, ALU.add).then_inc(ready, 1)

            def normalise(xn, x_, mv, rstd):
                for i in range(LT):
                    ins = nc.vector.tensor_scalar(xn[:, i, :], x_[:, i, :], mv[:, i, 0:1], rstd[:, i:i + 1],
                                                  ALU.subtract, ALU.mult)
                return ins

            def front_stats(b, half, par):
                dve.wait_ge(s_xf[par], 16 * (half + 1))
                variance(Steps(dve, v_ln1, LN1_STEPS, b), xf[par], st1, mv1, ve1, s_var1)

            def front_norm(b, half, par):
                dve.wait_ge(s_rstd1, b + 1)
                dve.wait_ge(s_mf[par], 16 * (half + 1))
                if not first(b):
                    dve.wait_ge(s_hs, b)
                normalise(xn1, xf[par], mv1, rs1).then_inc(s_xn1, 1)

            def front_pos(b, half, par):
                dve.wait_ge(s_posp, b + 1)
                nc.vector.tensor_tensor(pos[:, :], pf[0:Q, 0:G], posc[:, :], ALU.add).then_inc(s_pos, 1)
                nc.vector.tensor_tensor(fp[:, :, :].rearrange("p t a -> p (t a)"), pf[:, 128:128 + 2 * LT], fpc[:, :],
                                        ALU.add).then_inc(s_fpr, 1)
                dve.wait_ge(s_fpr, b + 1)
                st = Steps(dve, v_lin, LIN_STEPS, b)
                st.did(nc.vector.reciprocal(invf[:, :], fp[:, :, 0]))
                st.did(nc.vector.tensor_tensor(lp[:, :], lcol[:, :], fp[:, :, 1], ALU.add))
                st.wait()
                nc.vector.scalar_tensor_tensor(nlf[:, :], lp[:, :], -1.0, invf[:, :], ALU.mult, ALU.mult).then_inc(s_lin, 1)
                nc.vector.tensor_tensor(hclip[par][0:NX, :], pf[0:NX, 384:384 + C], own[:, :], ALU.mult).then_inc(s_hc, 1)

            def front_round(b):
                dve.wait_ge(a_ca, b + 1)
                nc.vector.tensor_scalar(cb_[:, :, :], ca_[:, :, :], -float(HALF), float(HALF), ALU.max,
                                        ALU.min).then_inc(v_cl, 1)
                dve.wait_ge(v_cl, b + 1)
                nc.vector.tensor_scalar(ca_[:, :, :], cb_[:, :, :], ROUND, ROUND, ALU.add, ALU.subtract).then_inc(s_rnd, 1)

            def front_kappa(b):
                if not first(b):
                    dve.wait_ge(s_prod, b)
                st = Steps(dve, v_kap, KAP_STEPS, b)
                for i in range(LT):
                    ins = nc.vector.tensor_scalar(posl[:, i, :], srow[:, :], fp[:, i, 0:1], lp[:, i:i + 1], ALU.mult, ALU.add)
                st.did(ins)
                st.wait()
                st.did(nc.vector.tensor_scalar(kl[:, :, :], posl[:, :, 0:LOW], 0.0, -1.0, ALU.min, ALU.max))
                st.did(nc.vector.tensor_scalar(kh[:, :, :], posl[:, :, S - HIGH:S], -float(L - 1), 0.0, ALU.add, ALU.max))
                st.wait()
                nc.vector.tensor_scalar(kh[:, :, :], kh[:, :, :], 1.0, None, ALU.min).then_inc(s_kap, 1)

            def front_scaled(b):
                dve.wait_ge(s_pos, b + 1)
                nc.vector.tensor_scalar(pos16[:, :], pos[:, :], MIDDLE, 0.5 / REACH, ALU.subtract, ALU.mult).then_inc(v_sel, 1)

            def front_dist(b):
                dve.wait_ge(v_sel, 2 * b + 1)
                nc.vector.tensor_tensor(
                    dist[:, :, :], pos16[:, :].rearrange("p (a g) -> p a g", a=1).to_broadcast([Q, NB, G]),
                    ctr[:, :].rearrange("p (j g) -> p j g", g=G), ALU.subtract).then_inc(v_sel, 1)

            def front_sel(b):
                dve.wait_ge(v_sel, 2 * b + 2)
                if not first(b):
                    dve.wait_ge(s_pp, NC * b)
                nc.vector.tensor_scalar(sel[:, :, :], dist[:, :, :], 0.0, None, ALU.is_equal).then_inc(s_sel, 1)

            def front_wm(b):
                dve.wait_ge(p_split, SPLIT * (b + 1))
                if not first(b):
                    dve.wait_ge(s_pp, NC * b)
                for k in range(NK):
                    ins = nc.vector.tensor_scalar(wm[:, :, k * PH:(k + 1) * PH], wp[:, :, :], kmask[:, k:k + 1], None,
                                                  ALU.mult)
                ins.then_inc(s_wm, 1)

            def front_clip(b):
                dve.wait_ge(s_prod, b + 1)
                if not first(b):
                    dve.wait_ge(s_clTp, b)
                nc.vector.tensor_reduce(clip[:, :, 0:H], pl[:, :, :].rearrange("p (t h) s -> p t h s", t=LT), AX.X, ALU.add)
                nc.vector.tensor_reduce(clip[:, :, H:NX], ph[:, :, :].rearrange("p (t h) s -> p t h s", t=LT), AX.X,
                                        ALU.add).then_inc(s_clip, 1)

            def mid_A(b, hp, m):
                if hp == 0 and m == 0:
                    dve.wait_ge(s_cT, b + 1)
                    if not first(b):
                        dve.wait_ge(s_attn, b)
                dve.wait_ge(s_pw, 8 * b + 2 * hp + m + 1)
                nc.vector.tensor_tensor(
                    A[:, m, 2 * hp:2 * hp + 2, :], pw[m][:, :].rearrange("p (h l) -> p h l", h=2),
                    cTm[:, m:m + 1, :].to_broadcast([P, 2, L]), ALU.mult).then_inc(s_A, 1)

            def back_x2(b, half, par):
                dve.wait_ge(s_xk[par], 16 * (half + 1))
                dve.wait_ge(s_mk[par], 16 * (half + 1))
                dve.wait_ge(s_y, b + 1)
                nc.vector.tensor_tensor(yg[:, :, :], y[:, :, :], mk[par][:, 0:1, :].to_broadcast([P, LT, C]),
                                        ALU.mult).then_inc(v_x2, 1)
                dve.wait_ge(v_x2, 2 * b + 1)
                nc.vector.tensor_tensor(x2[par][:, :, :], yg[:, :, :], xk[par][:, :, :], ALU.add).then_inc(v_x2, 1)

            def back_stats(b, half, par):
                dve.wait_ge(v_x2, 2 * b + 2)
                hold()
                variance(Steps(dve, v_ln2, LN2_STEPS, b), x2[par], st2, mv2, ve2, s_var2)

            def back_norm(b, half, par):
                dve.wait_ge(s_rstd2, b + 1)
                normalise(xn2, x2[par], mv2, rs2).then_inc(v_h2, 1)
                dve.wait_ge(v_h2, 2 * b + 1)
                nc.vector.tensor_tensor(xm2[:, :, :], xn2[:, :, :], mk[par][:, 2:3, :].to_broadcast([P, LT, C]),
                                        ALU.mult).then_inc(v_h2, 1)
                dve.wait_ge(v_h2, 2 * b + 2)
                nc.vector.tensor_tensor(h2[:, :, :], xm2[:, :, :], mk[par][:, 1:2, :].to_broadcast([P, LT, C]),
                                        ALU.add).then_inc(s_h2, 1)

            def back_logits(b):
                dve.wait_ge(s_lgp, b + 1)
                nc.vector.tensor_tensor(
                    lg[:, :, :], pk[:, L:L + LT * E].rearrange("p (t e) -> p t e", e=E),
                    rb[:, :].rearrange("p (a e) -> p a e", a=1).to_broadcast([P, LT, E]), ALU.add).then_inc(s_lg, 1)

            def back_top(b):
                dve.wait_ge(s_lg, b + 1)
                hold()
                st = Steps(dve, v_top, TOP_STEPS, b)
                for i in range(LT):
                    ins = nc.vector.max(top[:, i, :], lg[:, i, :])
                st.did(ins)
                st.wait()
                hold()
                for i in range(LT):
                    ins = nc.vector.max_index(topi[:, i, :], top[:, i, :], lg[:, i, :])
                st.did(ins)
                st.wait()
                st.did(nc.vector.tensor_copy(topf[:, :, :], topi[:, :, :]))
                st.wait()
                for i in range(LT):
                    ins = nc.vector.tensor_scalar(top1[:, i, :], erow[:, :], topf[:, i, 0:1], None, ALU.is_equal)
                st.did(ins)
                st.wait()
                if not first(b):
                    dve.wait_ge(s_mTp, b)
                for i in range(LT):
                    ins = nc.vector.scalar_tensor_tensor(mask[:, i, :], erow[:, :], topf[:, i, 1:2], top1[:, i, :],
                                                         ALU.is_equal, ALU.add)
                ins.then_inc(s_mask, 1)

            def back_hm(b, n):
                dve.wait_ge(s_mb, 4 * b + n + 1)
                nc.vector.tensor_tensor(
                    hm[:, 2 * n:2 * n + 2, :], pk[:, :].rearrange("p (e l) -> p e l", e=2),
                    h2T[:, :].rearrange("p (a l) -> p a l", a=1).to_broadcast([P, 2, L]), ALU.mult).then_inc(s_hm, 1)

            def back_out(b, half, par):
                dve.wait_ge(s_moe, b + 1)
                if not first(b, 2):
                    dve.wait_ge(s_out[par], 16 * half)
                nc.vector.tensor_tensor(moe[:, :, :], pz[:, 0:L].rearrange("p (t c) -> p t c", c=C),
                                        mk[par][:, 3:4, :].to_broadcast([P, LT, C]), ALU.mult).then_inc(v_out, 1)
                dve.wait_ge(v_out, b + 1)
                nc.vector.tensor_tensor(ob[par][:, :, :], moe[:, :, :], x2[par][:, :, :], ALU.add).then_inc(s_ob, 1)

            def iteration(run, run_buf):
                run(0, front_sel)
                run_buf(2, front_stats)
                run_buf(-1, back_x2)
                run_buf(-1, back_stats)
                run(0, front_kappa)
                run_buf(-1, back_norm)
                run_buf(-2, back_out)
                run_buf(1, front_pos)
                run(-1, back_logits)
                run(-1, back_top)
                run(1, front_scaled)
                run(1, front_round)
                run(1, front_dist)
                run(0, front_clip)
                run(-1, back_hm, 0)
                run(0, mid_A, 0, 0)
                run(0, mid_A, 0, 1)
                run(-1, back_hm, 1)
                run(0, mid_A, 1, 0)
                run(0, mid_A, 1, 1)
                run(-1, back_hm, 2)
                run(0, mid_A, 2, 0)
                run(0, mid_A, 2, 1)
                run(0, mid_A, 3, 0)
                run(0, mid_A, 3, 1)
                run(-1, back_hm, 3)
                run_buf(2, front_norm)
                run(1, front_wm)

            prologue()
            schedule(dve, iteration, -2, 2, 7, 17)

        @block.tensor
        def _(pe):
            mm = nc.tensor.matmul

            def prologue():
                pe.wait_ge(s_silc, 1)
                mm(pw[0][0:B, :], scT[:, :], wmod[:, 0:512], start=True, stop=True)
                mm(pw[1][0:B, 0:256], scT[:, :], wmod[:, 512:768], start=True, stop=True).then_inc(s_modp, 1)
                pe.wait_ge(s_const, 16 * (N_CONST - 1))
                pe.wait_ge(s_wts, 16 * N_WTS)
                pe.wait_ge(s_zero, N_ZERO)
                pe.wait_ge(s_esel, 1)
                pe.wait_ge(v_cast, 10)
                pe.wait_ge(s_modc, 2)

            def mid_select(b, n):
                g0, g1 = CHUNKS[n]
                if n == 0:
                    pe.wait_ge(s_sel, b + 1)
                    pe.wait_ge(s_wm, b + 1)
                if n >= 2 or not first(b):
                    pe.wait_ge(s_pick, NC * b + max(n - 1, 0))
                for g in range(g0, g1):
                    ins = mm(pp[n % 2][0:NB, (g - g0) * NK * PH:(g - g0 + 1) * NK * PH], sel[:, :, g],
                             wm[:, g, :], start=True, stop=True)
                ins.then_inc(s_pp, 1)

            def mid_expand(b, hp, m):
                n = 2 * hp + m
                if n == 0:
                    pe.wait_ge(s_pick, NC * b + NC)
                if n >= 2 or not first(b):
                    pe.wait_ge(s_A, 8 * b + n - 1)
                for part in range(NP):
                    x0 = part * H + 2 * hp
                    ins = mm(pw[m][:, :], expand[:, m * P:(m + 1) * P], pick[:, x0:x0 + 2, 0:L],
                             start=(part == 0), stop=(part == NP - 1))
                ins.then_inc(s_pw, 1)

            def mid_attend(b, half, par, m):
                if m == 0:
                    pe.wait_ge(s_clT, b + 1)
                    pe.wait_ge(s_hc, b + 1)
                    pe.wait_ge(s_hs, b + 1)
                pe.wait_ge(s_A, 8 * b + 7 + m)
                for a in range(2):
                    for j in range(H // 2):
                        hh = 2 * j + a
                        mm(pa[32 * j:32 * j + 32, 0:L], hs[par][:, m * H + hh, :], A[:, m, hh, :],
                           start=(m == 0 and a == 0), stop=False)
                if m == LT - 1:
                    for j in range(H // 2):
                        ins = mm(pa[32 * j:32 * j + 32, 0:L], hclip[par][:, 32 * j:32 * j + 32], clipT[par][:, :],
                                 start=False, stop=True)
                    ins.then_inc(s_attn, 1)

            def front_hT(b):
                pe.wait_ge(s_h, b + 1)
                if not first(b):
                    pe.wait_ge(s_cT, b)
                for i in range(LT):
                    ins = nc.tensor.transpose(pf[:, i * P:(i + 1) * P], h[:, i, :], ident[:, :])
                ins.then_inc(s_hTp, 1)

            def front_wave(b):
                pe.wait_ge(s_hT, b + 1)
                mm(pf[0:40, L:2 * L], wvT[:, :], hT[:, 0:L], start=True, stop=True).then_inc(s_wvp, 1)

            def front_pos(b):
                pe.wait_ge(s_ft, b + 1)
                for k in range(NK):
                    mm(pf[0:Q, 0:G], spread[:, k, :], ft[:, k * G:(k + 1) * G], start=(k == 0), stop=(k == NK - 1))
                for i in range(LT):
                    mm(pf[:, 128 + 2 * i:130 + 2 * i], ft[:, i * P:(i + 1) * P], mean[:, :], start=True, stop=True)
                for i in range(LT):
                    ins = mm(pf[0:NX, 384:384 + C], ends[:, i, :], h[:, i, :],
                             start=(i == 0), stop=(i == LT - 1))
                ins.then_inc(s_posp, 1)

            def front_project(b, n):
                if n == 2:
                    pe.wait_ge(s_w, H * b + 4)
                elif n == 0:
                    if not first(b):
                        pe.wait_ge(s_w, H * b)
                    if not first(b, MOE_LAG + 1):
                        pe.wait_ge(v_out, b - MOE_LAG)
                for head in (2 * n, 2 * n + 1):
                    j = head % 4
                    for k in range(NK):
                        lo = (NK - 1 - k) * S
                        ins = mm(pz[0:Q, j * G:(j + 1) * G], kwz[:, head, lo:lo + Q],
                                 hT[:, k * G:(k + 1) * G], start=(k == 0), stop=(k == NK - 1))
                if n % 2 == 1:
                    ins.then_inc(s_zp, 1)

            def front_rows(b, i):
                if i == 0:
                    pe.wait_ge(s_hc, b + 1)
                    pe.wait_ge(s_fpr, b + 1)
                elif not first(b):
                    pe.wait_ge(s_aoT, b)
                dst = (pf, pa)[i][:, 0:NW]
                mm(dst, hT[:, i * P:(i + 1) * P], kwl[:, :], start=True, stop=False)
                mm(dst, one[:, :], kbp[:, :], start=False, stop=True).then_inc(s_wlp, 1)

            def front_clT(b):
                pe.wait_ge(s_clip, b + 1)
                pe.wait_ge(s_wl, 2 * b + 2)
                for i in range(LT):
                    ins = nc.tensor.transpose(pa[0:NX, i * P:(i + 1) * P], clip[:, i, :], ident[:, :])
                ins.then_inc(s_clTp, 1)

            def front_cT(b):
                pe.wait_ge(s_c, b + 1)
                pe.wait_ge(s_wl, 2 * b + 1)
                for m in range(LT):
                    for i in range(LT):
                        ins = nc.tensor.transpose(pf[:, m * L + i * P:m * L + (i + 1) * P],
                                                  cc_[:, i, m * P:(m + 1) * P], ident[:, :])
                ins.then_inc(s_cTp, 1)

            def back_y(b):
                pe.wait_ge(s_aoT, b + 1)
                if not first(b):
                    pe.wait_ge(s_hm, 4 * b)
                for i in range(LT):
                    ins = mm(pk[:, L + i * C:L + (i + 1) * C], aoT[:, i * P:(i + 1) * P], owT[:, :], start=True, stop=True)
                ins.then_inc(s_yp, 1)

            def back_h2T(b):
                pe.wait_ge(s_h2, b + 1)
                for i in range(LT):
                    ins = nc.tensor.transpose(pk[:, i * P:(i + 1) * P], h2[:, i, :], ident[:, :])
                ins.then_inc(s_h2Tp, 1)

            def back_router(b):
                pe.wait_ge(s_h2T, b + 1)
                for i in range(LT):
                    ins = mm(pk[:, L + i * E:L + (i + 1) * E], h2T[:, i * P:(i + 1) * P], rwT[:, :], start=True, stop=True)
                ins.then_inc(s_lgp, 1)

            def back_mT(b):
                pe.wait_ge(s_mask, b + 1)
                for i in range(LT):
                    ins = nc.tensor.transpose(pk[0:E, i * P:(i + 1) * P], mask[:, i, :], ident[:, :])
                ins.then_inc(s_mTp, 1)

            def back_mb(b, n):
                if n == 0:
                    pe.wait_ge(s_mT, 2 * b + 2)
                    pe.wait_ge(s_lg, b + 1)
                else:
                    pe.wait_ge(s_hm, 4 * b + n)
                for j in range(2):
                    e = 2 * n + j
                    ins = mm(pk[:, j * L:(j + 1) * L], esel[:, e * P:(e + 1) * P], mkTb[:, :], start=True, stop=True)
                ins.then_inc(s_mb, 1)

            def back_experts(b, i):
                if i == 0:
                    pe.wait_ge(s_hm, 4 * b + 4)
                    pe.wait_ge(s_w, H * (min(b + MOE_LAG, B - 1) + 1 if isinstance(b, int) else b + MOE_LAG + 1))
                dst = pz[:, i * C:(i + 1) * C]
                for e in range(E):
                    mm(dst, hm[:, e, i * P:(i + 1) * P], weT[:, e, :], start=(e == 0), stop=False)
                ins = mm(dst, mkT[:, i * P:(i + 1) * P], eb[:, :], start=False, stop=True)
                if i == LT - 1:
                    ins.then_inc(s_moe, 1)

            def iteration(run, run_buf):
                run(0, mid_expand, 1, 0)
                run(0, mid_expand, 1, 1)
                run(-1, back_mb, 2)
                run(0, mid_expand, 2, 0)
                run(0, mid_expand, 2, 1)
                run(1, front_cT)
                run(0, mid_expand, 3, 0)
                run(0, mid_expand, 3, 1)
                run(-1, back_mb, 3)
                run_buf(0, mid_attend, 0)
                run_buf(0, mid_attend, 1)
                run(-1, back_experts, 0)
                run(0, back_y)
                run(1, mid_select, 0)
                run(1, mid_select, 1)
                run(2, front_hT)
                run(1, front_rows, 1)
                run(1, mid_select, 2)
                run(1, mid_select, 3)
                run(2, front_wave)
                run(-1, back_experts, 1)
                run(1, mid_select, 4)
                run(1, mid_select, 5)
                run(2, front_pos)
                run(0, back_h2T)
                run(1, mid_select, 6)
                run(1, mid_select, 7)
                run(0, back_router)
                run(2, front_project, 0)
                run(1, mid_select, 8)
                run(2, front_project, 1)
                run(2, front_rows, 0)
                run(1, mid_select, 9)
                run(1, mid_select, 10)
                run(0, back_mT)
                run(2, front_project, 2)
                run(1, mid_select, 11)
                run(1, mid_select, 12)
                run(2, front_project, 3)
                run(0, back_mb, 0)
                run(1, mid_expand, 0, 0)
                run(1, mid_expand, 0, 1)
                run(0, back_mb, 1)
                run(1, front_clT)

            prologue()
            schedule(pe, iteration, -2, 1, 7, 16)


def kernel(L0_attn_x, L0_attn_wave_w, L0_attn_wave_b, L0_attn_kernel_w, L0_attn_kernel_b, L0_attn_out_w,
           L0_ffn_router_w, L0_ffn_router_b, L0_ffn_expert_w, L0_ffn_expert_b, L0_c, L0_wmod):
    import concourse.bacc as bacc
    from concourse.bass_utils import run_bass_kernel_spmd

    a = lambda x: np.ascontiguousarray(np.asarray(x))
    K = L0_attn_kernel_w.shape[0] // H
    arrays = constants()
    arrays["x"] = a(L0_attn_x)
    arrays["kwT"] = a(np.asarray(L0_attn_kernel_w).reshape(H, K, C)[:, :S].transpose(2, 0, 1))
    arrays["kb"] = a(np.asarray(L0_attn_kernel_b).reshape(H, K)[:, :S].T)
    arrays["kbl"] = a(np.asarray(L0_attn_kernel_b).reshape(H, K)[:, :S].reshape(1, NW))
    arrays["wvT"] = a(np.asarray(L0_attn_wave_w).T)
    arrays["wvb"] = a(np.asarray(L0_attn_wave_b).reshape(2 * H, 1))
    arrays["owT"] = a(np.asarray(L0_attn_out_w).T)
    arrays["rwT"] = a(np.asarray(L0_ffn_router_w).T)
    arrays["rb"] = a(L0_ffn_router_b)
    arrays["weT"] = a(np.asarray(L0_ffn_expert_w).transpose(2, 0, 1))
    arrays["eb"] = a(L0_ffn_expert_b)
    arrays["cT"] = a(np.asarray(L0_c).T)
    arrays["wmod"] = a(L0_wmod)

    nc = bacc.Bacc("TRN2", target_bir_lowering=False, num_devices=1)
    t, feed = {}, {}
    for name, v in arrays.items():
        v = a(v)
        feed[f"in_{name}"] = v
        t[name] = nc.dram_tensor(f"in_{name}", v.shape, mybir.dt.from_np(v.dtype), kind="ExternalInput").ap()
    t["mod"] = nc.dram_tensor("mod_rows", (B, 6, C), F32, kind="Internal").ap()
    t["out"] = nc.dram_tensor("out_0", (B, L, C), F32, kind="ExternalOutput").ap()
    build(nc, t)
    r = run_bass_kernel_spmd(nc, [feed], core_ids=[0])
    return r.results[0]["out_0"]
```

```python
from contextlib import ExitStack

import numpy as np

import concourse.bass as bass
from concourse import mybir

ALU = mybir.AluOpType
ACT = mybir.ActivationFunctionType
AX = mybir.AxisListType
F32 = mybir.dt.float32
BF16 = mybir.dt.bfloat16
F16 = mybir.dt.float16

P = 128
B, L, C = 16, 256, 128
LT = L // P
H, D = 8, 16
S, HALF = 33, 16
NK = 3
G = -(-L // NK)
LP = NK * G
Q = NK * S
BLK = 6
NB = -(-L // BLK)
NP = 3
PH = NP * H
LOW, HIGH = 17, 19
SLOT = 64
NX = 2 * H
E = 8
NE = NP * E
EPS = 1e-5
FREQ_MID, FREQ_T = 8.5, 7.5
PHASE = 16.0
REACH = 3.73
MIDDLE = (L - 1) / 2
ROUND = 12582912.0
PER = 512 // (NK * PH)
CHUNKS = [(g, min(g + PER, G)) for g in range(0, G, PER)]
NC = len(CHUNKS)
NW = H * S
HG = 3
NG = -(-H // HG)


def constants():
    q = np.arange(Q)
    k, s = q // S, q % S - HALF
    g = np.arange(G)
    c = {}
    c["ident"] = np.eye(P, dtype=np.float32)
    ctr = np.repeat((BLK * np.arange(NB) + (BLK - 1) / 2 - MIDDLE) / (2 * REACH), G)
    c["ctr"] = np.broadcast_to(ctr, (Q, NB * G)).astype(np.float16)
    c["kmask"] = (k[:, None] == np.arange(NK)[None, :]).astype(np.float32)
    c["posc"] = (G * k[:, None] + g[None, :] + FREQ_MID * s[:, None]).astype(np.float32)
    st = np.zeros((40, NK, Q), np.float32)
    for kk in range(NK):
        st[0:H, kk, :] = (k == kk) * s * FREQ_T / H
        st[32:40, kk, :] = (k == kk) * PHASE / H
    c["spread"] = st.reshape(40, NK * Q)
    v = np.zeros((40, 2), np.float32)
    v[0:H, 0] = FREQ_T / H
    v[32:40, 1] = PHASE / H
    c["mean"] = v
    c["tscale"] = np.where(np.arange(40) < 32, 0.5, 1.0).astype(np.float32)[:, None]
    e = np.zeros((P, L), np.float32)
    e[np.arange(L) // BLK, np.arange(L)] = 1.0
    e[SLOT + np.arange(L) // BLK, np.arange(L)] = 1.0
    c["expand32"] = e
    c["mrow"] = np.broadcast_to(np.arange(L, dtype=np.float32), (P, L)).copy()
    c["lcol"] = (np.arange(P)[:, None] + P * np.arange(LT)[None, :]).astype(np.float32)
    c["fpc"] = np.broadcast_to(np.array([FREQ_MID, 0.0] * LT, np.float32), (P, 2 * LT)).copy()
    c["erow"] = np.broadcast_to(np.arange(NP * E, dtype=np.float32) % E, (P, NP * E)).copy()
    c["pmask"] = (np.arange(NP * E)[:, None] // E == np.arange(NP)[None, :]).astype(np.float32)
    c["srow"] = np.broadcast_to(np.arange(S, dtype=np.float32) - HALF, (P, S)).copy()
    ends = np.zeros((P, LT, NX), np.float32)
    ends[0, 0, :H] = 1.0
    ends[P - 1, LT - 1, H:] = 1.0
    c["ends"] = ends.reshape(P, LT * NX)
    own = (np.arange(NX)[:, None] % H == np.arange(C)[None, :] // D).astype(np.float32)
    c["own"] = own * np.where(np.arange(NX) < H, -1.0, 1.0).astype(np.float32)[:, None]
    esel = np.zeros((E, E, P), np.float32)
    esel[np.arange(E), np.arange(E), :] = 1.0
    c["esel"] = esel.reshape(E, E * P)
    return c


PACKS = {
    "early": (P, [("ident", P), ("wvT", 40), ("kwl", NW), ("mrow", L), ("ends", LT * NX), ("srow", S), ("lcol", LT),
                  ("fpc", 2 * LT)]),
    "selection": (Q, [("posc", G), ("kmask", NK), ("kb", NG)]),
    "wave": (40, [("spread", NK * Q), ("mean", 2), ("tscale", 1), ("wvb", 1)]),
    "late": (P, [("expand32", L), ("erow", NP * E), ("owT", P), ("rwT", E), ("weT", E * P)]),
    "experts": (NP * E, [("eb", C), ("pmask", NP)]),
}


def build(nc, t):
    ctx = ExitStack()
    with ctx:
        def sb(name, shape, dt=F32):
            return ctx.enter_context(nc.sbuf_tensor(name, shape, dt))

        def bank(name):
            return ctx.enter_context(nc.psum_tensor(name, [P, 512], F32))

        def sem(name):
            return ctx.enter_context(nc.semaphore(name))

        packs, at = {}, {}
        for pack, (rows, columns) in PACKS.items():
            packs[pack] = sb(pack, [rows, sum(n for _, n in columns)])
            c0 = 0
            for name, n in columns:
                at[name] = packs[pack][:, c0:c0 + n]
                c0 += n
        ident, wvT, kwl, mrow, srow, lcol, fpc = (at[n] for n in ("ident", "wvT", "kwl", "mrow", "srow", "lcol", "fpc"))
        ends = at["ends"].rearrange("p (t x) -> p t x", t=LT)
        posc, kmask, kb, mean, tscale, wvb = (at[n] for n in ("posc", "kmask", "kb", "mean", "tscale", "wvb"))
        spread = at["spread"].rearrange("p (k q) -> p k q", k=NK)
        expand32, erow, owT, rwT, eb, pmask = (at[n] for n in ("expand32", "erow", "owT", "rwT", "eb", "pmask"))
        weT = at["weT"].rearrange("p (e c) -> p e c", e=E)
        ctr = sb("ctr", [Q, NB * G], F16)
        expand = sb("expand", [P, L], BF16)
        own = sb("own", [NX, C])
        kbl = sb("kbl", [NP, NW]); kbr = sb("kbr", [NP, NW]); kbs = sb("kbs", [NP, NP, NW], BF16)
        kbt = sb("kbt", [NP, 2, NW], BF16); kbp = sb("kbp", [NP, NW], BF16)
        one = sb("one", [NP, P], BF16)
        esel32 = sb("esel32", [E, E * P])
        esel = sb("esel", [E, E * P], BF16)
        rb = sb("rb", [P, E])
        ebr = sb("ebr", [NE, C]); ebs = sb("ebs", [NE, NP, C], BF16)
        ebt = sb("ebt", [NE, 2, C], BF16); ebp = sb("ebp", [NE, C], BF16)
        cT = sb("cT", [P, B])
        scT = sb("scT", [P, B])
        wmod = sb("wmod", [P, 6 * C])
        mod = sb("mod", [B, 6 * C])
        gsign = sb("gsign", [B, 2, C]); gabs = sb("gabs", [B, 2, C])
        mhalf = sb("mhalf", [P, LT])
        spare = sb("spare", [P, 1])
        xf = [sb(f"xf{i}", [P, LT, C]) for i in range(2)]
        xk = [sb(f"xk{i}", [P, LT, C]) for i in range(2)]
        mf = [sb(f"mf{i}", [P, 2, C]) for i in range(2)]
        mk = [sb(f"mk{i}", [P, 4, C]) for i in range(2)]
        st1 = sb("st1", [P, LT, 6]); mv1 = sb("mv1", [P, LT, 2]); rs1 = sb("rs1", [P, LT]); ve1 = sb("ve1", [P, LT])
        xn1 = sb("xn1", [P, LT, C]); xm1 = sb("xm1", [P, LT, C])
        hs = [sb(f"hs{i}", [P, LT * H, 2 * D]) for i in range(2)]
        h = sb("h", [P, LT, C]); hT = sb("hT", [P, LP])
        wv = sb("wv", [40, L])
        ft = sb("ft", [40, LP])
        pos = sb("pos", [Q, G])
        pos16 = sb("pos16", [Q, G], F16)
        dist = sb("dist", [Q, NB, G], mybir.dt.int16)
        sel = sb("sel", [Q, SLOT + NB, G], BF16)
        wT = sb("wT", [HG * S, NG, L]); w = sb("w", [Q, H, G])
        wr = sb("wr", [Q, G, H]); wp = sb("wp", [Q, G, PH], BF16)
        wm = sb("wm", [Q, G, NK * PH], BF16)
        wl = sb("wl", [P, LT, NW]); posl = sb("posl", [P, LT, S])
        kl = sb("kl", [P, LT, LOW]); kh = sb("kh", [P, LT, HIGH])
        pl = sb("pl", [P, LT * H, LOW]); ph = sb("ph", [P, LT * H, HIGH])
        clip = sb("clip", [P, LT, NX])
        clipT = [sb(f"clipT{i}", [P, L]) for i in range(2)]
        fp = sb("fp", [P, LT, 2]); invf = sb("invf", [P, LT]); lp = sb("lp", [P, LT]); nlf = sb("nlf", [P, LT])
        ca_ = sb("ca_", [P, LT, L]); cb_ = sb("cb_", [P, LT, L])
        cc_ = sb("cc_", [P, LT, L])
        cTm = sb("cTm", [P, LT, L])
        hclip = [sb(f"hclip{i}", [P, C]) for i in range(2)]
        pick = sb("pick", [P, 2 * H, LP], BF16)
        A = sb("A", [P, LT, H, L])
        aoT = sb("aoT", [P, L])
        y = sb("y", [P, LT, C]); yg = sb("yg", [P, LT, C]); x2 = [sb(f"x2{i}", [P, LT, C]) for i in range(2)]
        st2 = sb("st2", [P, LT, 6]); mv2 = sb("mv2", [P, LT, 2]); rs2 = sb("rs2", [P, LT]); ve2 = sb("ve2", [P, LT])
        xn2 = sb("xn2", [P, LT, C]); xm2 = sb("xm2", [P, LT, C]); h2 = sb("h2", [P, LT, C])
        h2T = sb("h2T", [P, L])
        lg = sb("lg", [P, LT, E])
        top = sb("top", [P, LT, E]); topi = sb("topi", [P, LT, E], mybir.dt.uint32)
        topf = sb("topf", [P, LT, E]); top1 = sb("top1", [P, LT, NE]); mask = sb("mask", [P, LT, NE])
        mkT = sb("mkT", [NE, L], BF16)
        hm = sb("hm", [P, E, L])
        moe = sb("moe", [P, LT, C])
        ob = [sb(f"ob{i}", [P, LT, C]) for i in range(2)]

        pw = [bank("pw0"), bank("pw1")]
        pp = [bank("pp0"), bank("pp1")]
        pk = bank("pk")
        pz = bank("pz")
        pf = bank("pf")
        pa = bank("pa")

        s_const = sem("s_const")
        s_zero = sem("s_zero")
        s_wmod = sem("s_wmod")
        s_silc = sem("s_silc"); s_modp = sem("s_modp"); s_modc = sem("s_modc"); s_gate = sem("s_gate")
        s_mod = sem("s_mod"); s_modd = sem("s_modd")
        s_xf = [sem(f"s_xf{i}") for i in range(2)]
        s_mf = [sem(f"s_mf{i}") for i in range(2)]
        s_xk = [sem(f"s_xk{i}") for i in range(2)]
        s_mk = [sem(f"s_mk{i}") for i in range(2)]
        s_out = [sem(f"s_out{i}") for i in range(2)]
        s_biases = sem("s_biases")
        v_cast = sem("v_cast"); s_cast = sem("s_cast")
        v_ln1 = sem("v_ln1")
        s_var1 = sem("s_var1"); s_rstd1 = sem("s_rstd1")
        s_var2 = sem("s_var2"); s_rstd2 = sem("s_rstd2")
        s_xn1 = sem("s_xn1"); p_xm1 = sem("p_xm1")
        s_h = sem("s_h")
        s_hs = sem("s_hs")
        s_hTp = sem("s_hTp"); s_hT = sem("s_hT")
        s_wvp = sem("s_wvp"); a_wv = sem("a_wv"); s_ft = sem("s_ft")
        s_posp = sem("s_posp")
        s_hc = sem("s_hc")
        s_pos = sem("s_pos")
        s_fpr = sem("s_fpr")
        v_lin = sem("v_lin"); s_lin = sem("s_lin")
        a_ca = sem("a_ca"); v_cl = sem("v_cl"); s_rnd = sem("s_rnd"); a_cb = sem("a_cb"); p_cc = sem("p_cc")
        a_c = sem("a_c"); s_c = sem("s_c"); s_cTp = sem("s_cTp"); s_cT = sem("s_cT")
        v_sel = sem("v_sel"); s_sel = sem("s_sel"); s_sel2 = sem("s_sel2")
        s_zp = sem("s_zp"); s_wT = sem("s_wT")
        s_wd = sem("s_wd"); s_w = sem("s_w")
        s_part = sem("s_part"); s_rest = sem("s_rest")
        s_wm = sem("s_wm")
        s_wlp = sem("s_wlp"); s_wl = sem("s_wl")
        v_kap = sem("v_kap"); s_kap = sem("s_kap"); s_prod = sem("s_prod"); s_clip = sem("s_clip")
        s_clTp = sem("s_clTp"); s_clT = sem("s_clT")
        s_pp = sem("s_pp"); s_pick = sem("s_pick")
        s_pw = sem("s_pw"); s_A = sem("s_A"); s_attn = sem("s_attn")
        s_aoT = sem("s_aoT")
        s_yp = sem("s_yp"); s_y = sem("s_y")
        p_yg = sem("p_yg"); s_x2 = sem("s_x2"); v_ln2 = sem("v_ln2"); s_xn2 = sem("s_xn2"); p_xm2 = sem("p_xm2"); s_h2 = sem("s_h2")
        s_h2Tp = sem("s_h2Tp"); s_h2T = sem("s_h2T")
        s_lgp = sem("s_lgp"); s_lg = sem("s_lg"); v_top = sem("v_top"); s_mask = sem("s_mask")
        s_mTp = sem("s_mTp"); s_mT = sem("s_mT"); s_mb = sem("s_mb"); s_hm = sem("s_hm")
        s_moe = sem("s_moe"); s_gated = sem("s_gated"); s_ob = sem("s_ob")

        block = ctx.enter_context(nc.Block())

        class Steps:
            def __init__(self, eng, semaphore, per, b):
                self.eng, self.sem, self.per, self.b, self.k = eng, semaphore, per, b, 0

            def did(self, ins):
                ins.then_inc(self.sem, 1)
                self.k += 1
                assert self.k <= self.per

            def wait(self):
                self.eng.wait_ge(self.sem, self.b * self.per + self.k)

        def hold():
            nc.vector.memset(spare[:, :], 0.0)

        LN1_STEPS, LN2_STEPS, LIN_STEPS, KAP_STEPS, TOP_STEPS = 2, 2, 2, 3, 4
        MOE_LAG = 3

        COL = (0, 2 * H, H)

        def heads(j):
            return min(HG, H - HG * j)

        def first(b, n=1):
            return isinstance(b, int) and b < n

        w_of = w[:, :, :].rearrange("q h g -> q g h")

        def h_of(par):
            return hs[par][:, :, :].rearrange("p (x a) (q d) -> p x (a q) d", a=2, q=2)[:, :, 0:4:3, :]

        def schedule(eng, iteration, i0, r0, r1, i1):
            def steps(i, r):
                def run_buf(lag, stage, *args):
                    n = i + lag
                    if r is not None:
                        stage(2 * r + n, r + n // 2, n % 2, *args)
                    elif 0 <= n < B:
                        stage(n, n // 2, n % 2, *args)

                def run(lag, stage, *args):
                    run_buf(lag, lambda b, half, par: stage(b, *args))
                iteration(run, run_buf)

            for i in range(i0, 2 * r0):
                steps(i, None)
            with eng.Fori(r0, r1) as r:
                steps(0, r)
                steps(1, r)
            for i in range(2 * r1, i1 + 1):
                steps(i, None)

        N_CONST = 7

        @block.sync
        def _(sp):
            def load_x(b, par):
                sp.dma_start(xf[par][:, :, :], t["x"][bass.ds(b, 1)].rearrange("a (t p) c -> p (a t) c", p=P)).then_inc(s_xf[par], 16)

            def load_mf(b, par):
                sp.dma_start(mf[par][:, :, :], t["mod"][bass.ds(b, 1), 0:2].to_broadcast([P, 2, C])).then_inc(s_mf[par], 16)

            def load_front(b, par):
                load_x(b, par)
                load_mf(b, par)

            def load_back(b, par):
                sp.dma_start(xk[par][:, :, :], t["x"][bass.ds(b, 1)].rearrange("a (t p) c -> p (a t) c", p=P)).then_inc(s_xk[par], 16)
                sp.dma_start(mk[par][:, :, :], t["mod"][bass.ds(b, 1), 2:6].to_broadcast([P, 4, C])).then_inc(s_mk[par], 16)

            def constant(dst, src):
                sp.dma_start(dst, src).then_inc(s_const, 16)

            for dst, name in ((cT[:, :], "cT"), (wmod[:, :], "wmod")):
                sp.dma_start(dst, t[name]).then_inc(s_wmod, 16)
            load_x(0, 0)
            for dst, src in ((packs["early"][:, :], t["early"]), (packs["experts"][:, :], t["experts"]),
                             (kbl[:, :], t["kbl"].to_broadcast([NP, NW]))):
                sp.dma_start(dst, src).then_inc(s_biases, 16)
            for pack in ("wave", "selection"):
                constant(packs[pack][:, :], t[pack])
            constant(ctr[:, :], t["ctr"])
            constant(own[:, :], t["own"])
            constant(packs["late"][:, :], t["late"])
            sp.wait_ge(s_mod, 3)
            sp.dma_start(t["mod"].rearrange("b s c -> b (s c)"), mod[:, :]).then_inc(s_modd, 16)
            constant(rb[:, :], t["rb"].rearrange("(a e) -> a e", a=1).to_broadcast([P, E]))
            constant(esel32[:, :], t["esel"])
            sp.wait_ge(s_modd, 16)

            load_mf(0, 0)
            load_front(1, 1)
            load_back(0, 0)
            load_back(1, 1)

            def ahead(b):
                return not isinstance(b, int) or b + 2 < B

            def after_h(b, half, par):
                if ahead(b):
                    sp.wait_ge(s_hs, b + 1)
                    load_front(b + 2, par)

            def after_out(b, half, par):
                sp.wait_ge(s_ob, b + 1)
                sp.dma_start(t["out"][bass.ds(b, 1)].rearrange("a (t p) c -> p (a t) c", p=P),
                             ob[par][:, :, :]).then_inc(s_out[par], 16)
                if ahead(b):
                    load_back(b + 2, par)

            def weights(b):
                sp.wait_ge(s_wT, NG * (b + 1))
                for j in range(NG):
                    n = heads(j) * S
                    sp.dma_start(t["weights"][HG * S * j:HG * S * j + n], wT[0:n, j, :]).then_inc(s_wd, 16)
                sp.wait_ge(s_wd, 16 * NG * (b + 1))
                if not first(b):
                    sp.wait_ge(s_rest, 2 * b - 1)
                for k in range(NK):
                    n = min(G, L - k * G)
                    sp.dma_start(w[k * S:(k + 1) * S, :, 0:n], t["weights"][:, k * G:k * G + n].rearrange(
                        "(h s) g -> s h g", s=S)).then_inc(s_w, 16)

            def iteration(run, run_buf):
                run(2, weights)
                run_buf(2, after_h)
                run_buf(-1, after_out)

            schedule(sp, iteration, -2, 1, 6, 16)
            for p_ in range(2):
                sp.wait_ge(s_out[p_], 16 * B // 2)

        N_ZERO = 11

        @block.gpsimd
        def _(pool):
            nc.gpsimd.memset(w[:, :, :], 0.0).then_inc(s_zero, 1)
            nc.gpsimd.memset(mhalf[:, :], -0.5).then_inc(s_zero, 1)
            nc.gpsimd.memset(sel[:, NB:SLOT, :], 0.0).then_inc(s_zero, 1)
            nc.gpsimd.memset(hs[0][:, :, :], 0.0).then_inc(s_zero, 1)
            nc.gpsimd.memset(hs[1][:, :, :], 0.0).then_inc(s_zero, 1)
            nc.gpsimd.memset(hT[:, L:LP], 0.0).then_inc(s_zero, 1)
            nc.gpsimd.memset(ft[:, L:LP], 0.0).then_inc(s_zero, 1)
            nc.gpsimd.memset(hclip[0][:, :], 0.0).then_inc(s_zero, 1)
            nc.gpsimd.memset(hclip[1][:, :], 0.0).then_inc(s_zero, 1)
            nc.gpsimd.memset(clipT[0][:, :], 0.0).then_inc(s_zero, 1)
            nc.gpsimd.memset(clipT[1][:, :], 0.0).then_inc(s_zero, 1)
            pool.wait_ge(s_biases, 16 * 3)
            pool.wait_ge(s_const, 16 * N_CONST)
            pool.wait_ge(s_zero, N_ZERO)

            def front_rstd(b):
                pool.wait_ge(s_var1, b + 1)
                nc.gpsimd.tensor_tensor(rs1[:, :], ve1[:, :], mhalf[:, :], ALU.pow).then_inc(s_rstd1, 1)

            def back_rstd(b):
                pool.wait_ge(s_var2, b + 1)
                nc.gpsimd.tensor_tensor(rs2[:, :], ve2[:, :], mhalf[:, :], ALU.pow).then_inc(s_rstd2, 1)

            def front_h(b, half, par):
                pool.wait_ge(s_xn1, b + 1)
                nc.gpsimd.tensor_tensor(xm1[:, :, :], xn1[:, :, :], mf[par][:, 1:2, :].to_broadcast([P, LT, C]),
                                        ALU.mult).then_inc(p_xm1, 1)
                pool.wait_ge(p_xm1, b + 1)
                if not first(b):
                    pool.wait_ge(s_posp, b)
                nc.gpsimd.tensor_tensor(h[:, :, :], xm1[:, :, :], mf[par][:, 0:1, :].to_broadcast([P, LT, C]),
                                        ALU.add).then_inc(s_h, 1)

            def front_hs(b, half, par):
                pool.wait_ge(s_h, b + 1)
                if not first(b, 2):
                    pool.wait_ge(s_attn, b - 1)
                for i in range(LT):
                    ins = nc.gpsimd.tensor_tensor(
                        h_of(par)[:, i * H // 2:(i + 1) * H // 2],
                        xm1[:, i, :].rearrange("p (j a d) -> p j a d", a=2, d=D),
                        mf[par][:, 0, :].rearrange("p (j a d) -> p j a d", a=2, d=D), ALU.add)
                ins.then_inc(s_hs, 1)

            def front_dist(b):
                pool.wait_ge(a_cb, b + 1)
                if not first(b):
                    pool.wait_ge(s_cTp, b)
                nc.gpsimd.tensor_tensor(cc_[:, :, :], cb_[:, :, :],
                                        mrow[:, :].rearrange("p (a l) -> p a l", a=1).to_broadcast([P, LT, L]),
                                        ALU.subtract).then_inc(p_cc, 1)

            def front_split(b, step):
                pool.wait_ge(s_part, 2 * b + step + 1)
                src, rest = ((w_of, wr[:, :, :]), (wr[:, :, :], wp[:, :, COL[2]:COL[2] + H]))[step]
                nc.gpsimd.tensor_tensor(rest, src, wp[:, :, COL[step]:COL[step] + H],
                                        ALU.subtract).then_inc(s_rest, 1)

            def back_x2(b, half, par):
                pool.wait_ge(s_xk[par], 16 * (half + 1))
                pool.wait_ge(s_mk[par], 16 * (half + 1))
                pool.wait_ge(s_y, b + 1)
                nc.gpsimd.tensor_tensor(yg[:, :, :], y[:, :, :], mk[par][:, 0:1, :].to_broadcast([P, LT, C]),
                                        ALU.mult).then_inc(p_yg, 1)
                pool.wait_ge(p_yg, b + 1)
                nc.gpsimd.tensor_tensor(x2[par][:, :, :], yg[:, :, :], xk[par][:, :, :], ALU.add).then_inc(s_x2, 1)

            def back_h2(b, half, par):
                pool.wait_ge(s_xn2, b + 1)
                nc.gpsimd.tensor_tensor(xm2[:, :, :], xn2[:, :, :], mk[par][:, 2:3, :].to_broadcast([P, LT, C]),
                                        ALU.mult).then_inc(p_xm2, 1)
                pool.wait_ge(p_xm2, b + 1)
                if not first(b):
                    pool.wait_ge(s_h2Tp, b)
                nc.gpsimd.tensor_tensor(h2[:, :, :], xm2[:, :, :], mk[par][:, 1:2, :].to_broadcast([P, LT, C]),
                                        ALU.add).then_inc(s_h2, 1)

            def back_add(b, half, par):
                pool.wait_ge(s_gated, b + 1)
                if not first(b, 2):
                    pool.wait_ge(s_out[par], 16 * half)
                nc.gpsimd.tensor_tensor(ob[par][:, :, :], moe[:, :, :], x2[par][:, :, :], ALU.add).then_inc(s_ob, 1)

            def front_prod(b):
                pool.wait_ge(s_kap, b + 1)
                pool.wait_ge(s_wl, 2 * b + 2)
                if not first(b):
                    pool.wait_ge(s_clip, b)
                for i in range(LT):
                    wrow = wl[:, i, :].rearrange("p (h s) -> p h s", s=S)
                    nc.gpsimd.tensor_tensor(pl[:, i * H:(i + 1) * H, :], wrow[:, :, 0:LOW],
                                            kl[:, i:i + 1, :].to_broadcast([P, H, LOW]), ALU.mult)
                    ins = nc.gpsimd.tensor_tensor(ph[:, i * H:(i + 1) * H, :], wrow[:, :, S - HIGH:S],
                                                  kh[:, i:i + 1, :].to_broadcast([P, H, HIGH]), ALU.mult)
                ins.then_inc(s_prod, 1)

            def iteration(run, run_buf):
                run_buf(-1, back_h2)
                run(1, front_dist)
                run(1, front_split, 0)
                run(1, front_split, 1)
                run_buf(2, front_hs)
                run(1, front_prod)
                run(3, front_rstd)
                run_buf(-2, back_add)
                run_buf(3, front_h)
                run_buf(0, back_x2)
                run(0, back_rstd)

            schedule(pool, iteration, -3, 2, 6, 17)

        @block.scalar
        def _(act):
            def prologue():
                act.wait_ge(s_wmod, 32)
                nc.scalar.activation(scT[:, :], cT[:, :], ACT.Silu).then_inc(s_silc, 1)
                act.wait_ge(s_modp, 1)
                nc.scalar.activation(mod[:, 0:512], pw[0][0:B, :], ACT.Copy).then_inc(s_modc, 1)
                nc.scalar.activation(mod[:, 512:768], pw[1][0:B, 0:256], ACT.Copy).then_inc(s_modc, 1)
                act.wait_ge(s_biases, 16 * 3)
                act.wait_ge(s_const, 16 * N_CONST)
                nc.scalar.activation(expand[:, :], expand32[:, :], ACT.Copy).then_inc(s_cast, 1)
                nc.scalar.activation(esel[:, :], esel32[:, :], ACT.Copy).then_inc(s_cast, 1)

            def back_aoT(b):
                act.wait_ge(s_attn, b + 1)
                nc.scalar.activation(aoT[:, :], pa[:, 0:L], ACT.Copy).then_inc(s_aoT, 1)

            def mid_pick(b, n):
                g0, g1 = CHUNKS[n]
                act.wait_ge(s_pp, NC * b + n + 1)
                if n == 0 and not first(b):
                    act.wait_ge(s_pw, 8 * b)
                src = pp[n % 2][:, 0:(g1 - g0) * NK * PH].rearrange("p (g k x) -> p g k x", k=NK, x=PH)
                dst = pick[:, :, :].rearrange("p x (k g) -> p g k x", g=G)[:, g0:g1]
                nc.scalar.activation(dst[0:NB], src[0:NB, :, :, 0:2 * H], ACT.Copy)
                nc.scalar.activation(dst[SLOT:SLOT + NB, :, :, 0:H], src[SLOT:SLOT + NB, :, :, 2 * H:PH],
                                     ACT.Copy).then_inc(s_pick, 1)

            def back_y(b):
                act.wait_ge(s_yp, b + 1)
                nc.scalar.activation(y[:, :, :].rearrange("p t c -> p (t c)"), pk[:, L:2 * L], ACT.Silu).then_inc(s_y, 1)

            def front_hT(b):
                act.wait_ge(s_hTp, b + 1)
                if not first(b):
                    act.wait_ge(s_zp, 2 * b)
                    act.wait_ge(s_wlp, 2 * b)
                nc.scalar.activation(hT[:, 0:L], pf[:, 0:L], ACT.Copy).then_inc(s_hT, 1)

            def front_wave(b):
                act.wait_ge(s_wvp, b + 1)
                nc.scalar.activation(wv[:, :], pf[0:40, L:2 * L], ACT.Silu, bias=wvb[:, 0:1]).then_inc(a_wv, 1)
                act.wait_ge(a_wv, b + 1)
                nc.scalar.activation(ft[:, 0:L], wv[:, :], ACT.Tanh, scale=tscale[:, 0:1]).then_inc(s_ft, 1)

            def back_h2T(b):
                act.wait_ge(s_h2Tp, b + 1)
                nc.scalar.activation(h2T[:, :], pk[:, 0:L], ACT.Copy).then_inc(s_h2T, 1)

            def front_w(b, step):
                act.wait_ge(s_zp, 2 * b + step + 1)
                if step == 0 and not first(b):
                    act.wait_ge(s_wd, 16 * NG * b)
                for j in ((0, 1), (2,))[step]:
                    n = heads(j) * S
                    nc.scalar.activation(wT[0:n, j, :], pz[0:n, j % 2 * L:(j % 2 + 1) * L], ACT.Silu,
                                         bias=kb[0:n, j:j + 1]).then_inc(s_wT, 1)

            def front_part(b, n):
                if n == 0:
                    act.wait_ge(s_w, 16 * NK * (b + 1))
                    if not first(b):
                        act.wait_ge(s_wm, b)
                else:
                    act.wait_ge(s_rest, 2 * b + 1)
                nc.scalar.activation(wp[:, :, COL[n]:COL[n] + H], (w_of, wr[:, :, :])[n], ACT.Copy).then_inc(s_part, 1)

            def front_sel2(b, half):
                j0, j1 = ((0, NB // 2), (NB // 2, NB))[half]
                act.wait_ge(s_sel, b + 1)
                nc.scalar.activation(sel[:, SLOT + j0:SLOT + j1, :], sel[:, j0:j1, :], ACT.Copy).then_inc(s_sel2, 1)

            def front_wl(b, i):
                act.wait_ge(s_wlp, 2 * b + i + 1)
                if i == 0 and not first(b):
                    act.wait_ge(s_prod, b)
                nc.scalar.activation(wl[:, i, :], (pf, pa)[i][:, 0:NW], ACT.Silu).then_inc(s_wl, 1)

            def front_number(b):
                act.wait_ge(s_lin, b + 1)
                for i in range(LT):
                    ins = nc.scalar.activation(ca_[:, i, :], mrow[:, :], ACT.Identity, bias=nlf[:, i:i + 1],
                                               scale=invf[:, i:i + 1])
                ins.then_inc(a_ca, 1)

            def front_near(b):
                act.wait_ge(s_rnd, b + 1)
                for i in range(LT):
                    ins = nc.scalar.activation(cb_[:, i, :], ca_[:, i, :], ACT.Identity, bias=lp[:, i:i + 1],
                                               scale=fp[:, i, 0:1])
                ins.then_inc(a_cb, 1)

            def front_c(b):
                act.wait_ge(p_cc, b + 1)
                nc.scalar.activation(cc_[:, :, :], cc_[:, :, :], ACT.Abs).then_inc(a_c, 1)
                act.wait_ge(a_c, b + 1)
                nc.scalar.activation(cc_[:, :, :], cc_[:, :, :], ACT.Relu, bias=1.0, scale=-1.0).then_inc(s_c, 1)

            def front_clT(b, half, par):
                act.wait_ge(s_clTp, b + 1)
                nc.scalar.activation(clipT[par][0:NX, :], pa[0:NX, 0:L], ACT.Copy).then_inc(s_clT, 1)

            def front_cT(b):
                act.wait_ge(s_cTp, b + 1)
                if not first(b):
                    act.wait_ge(s_A, 8 * b)
                nc.scalar.activation(cTm[:, :, :].rearrange("p t l -> p (t l)"), pf[:, :], ACT.Copy).then_inc(s_cT, 1)

            def back_mT(b):
                act.wait_ge(s_mTp, b + 1)
                nc.scalar.activation(mkT[:, :], pk[0:NE, 0:L], ACT.Copy).then_inc(s_mT, 1)

            def iteration(run, run_buf):
                run(0, front_cT)
                run(0, front_wl, 1)
                run(1, front_hT)
                run(0, mid_pick, 0)
                run(0, mid_pick, 1)
                run(0, mid_pick, 2)
                run(1, front_wave)
                run(0, mid_pick, 3)
                run(0, mid_pick, 4)
                run(1, front_w, 0)
                run(0, mid_pick, 5)
                run(0, mid_pick, 6)
                run(1, front_w, 1)
                run(0, mid_pick, 7)
                run(0, mid_pick, 8)
                run(-1, back_y)
                run(1, front_number)
                run(0, mid_pick, 9)
                run(0, mid_pick, 10)
                run_buf(0, front_clT)
                run(0, mid_pick, 11)
                run(0, mid_pick, 12)
                run(1, front_near)
                run(1, front_sel2, 0)
                run(1, front_part, 0)
                run(-1, back_h2T)
                run(1, front_sel2, 1)
                run(1, front_part, 1)
                run(1, front_wl, 0)
                run(1, front_c)
                run(0, back_aoT)
                run(-1, back_mT)

            prologue()
            schedule(act, iteration, -1, 1, 7, 16)

        @block.vector
        def _(dve):
            def prologue():
                cast.did(nc.vector.memset(pick[:, :, :], 0.0))
                cast.did(nc.vector.memset(one[:, :], 1.0))
                dve.wait_ge(s_modc, 2)
                m6 = mod[:, :].rearrange("p (s c) -> p s c", c=C)
                gates = m6[:, 2:6:3, :]
                scales = m6[:, 1:5:3, :]
                nc.vector.tensor_scalar(gsign[:, :, :], gates, 0.0, 2.0, ALU.is_ge, ALU.mult).then_inc(s_gate, 1)
                nc.vector.tensor_scalar(scales, scales, 1.0, None, ALU.add).then_inc(s_mod, 1)
                dve.wait_ge(s_gate, 1)
                nc.vector.scalar_tensor_tensor(gabs[:, :, :], gates, -1.0, gates, ALU.mult, ALU.max).then_inc(s_gate, 1)
                dve.wait_ge(s_gate, 2)
                nc.vector.tensor_scalar(gabs[:, :, :], gabs[:, :, :], 0.25, None, ALU.max).then_inc(s_mod, 1)
                dve.wait_ge(s_mod, 2)
                nc.vector.scalar_tensor_tensor(gates, gsign[:, :, :], -1.0, gabs[:, :, :], ALU.add, ALU.mult).then_inc(s_mod, 1)
                dve.wait_ge(s_biases, 16 * 3)
                parts_on_partitions(kbl, kbr, kbs, kbt, kbp, ident[0:NP, 0:NP])
                parts_on_partitions(eb, ebr, ebs, ebt, ebp, pmask[:, :])
                dve.wait_ge(s_const, 16 * N_CONST)

            cast = Steps(dve, v_cast, 16, 0)

            def parts_on_partitions(x_, rest, parts, sums, out, of_part):
                cast.did(nc.vector.tensor_copy(parts[:, 0, :], x_[:, :]))
                cast.wait()
                cast.did(nc.vector.tensor_tensor(rest[:, :], x_[:, :], parts[:, 0, :], ALU.subtract))
                cast.wait()
                cast.did(nc.vector.tensor_copy(parts[:, 1, :], rest[:, :]))
                cast.wait()
                cast.did(nc.vector.tensor_tensor(parts[:, 2, :], rest[:, :], parts[:, 1, :], ALU.subtract))
                cast.did(nc.vector.tensor_scalar(sums[:, 0, :], parts[:, 0, :], of_part[:, 0:1], None, ALU.mult))
                cast.wait()
                cast.did(nc.vector.scalar_tensor_tensor(sums[:, 1, :], parts[:, 1, :], of_part[:, 1:2], sums[:, 0, :],
                                                        ALU.mult, ALU.add))
                cast.wait()
                cast.did(nc.vector.scalar_tensor_tensor(out[:, :], parts[:, 2, :], of_part[:, 2:3], sums[:, 1, :],
                                                        ALU.mult, ALU.add))

            def variance(st, x_, stats, mv, ve, ready):
                for i in range(LT):
                    ins = nc.vector.bn_stats(stats[:, i, :], x_[:, i, :])
                st.did(ins)
                st.wait()
                hold()
                for i in range(LT):
                    ins = nc.vector.bn_aggr(mv[:, i, :], stats[:, i, :])
                st.did(ins)
                st.wait()
                nc.vector.tensor_scalar(ve[:, :], mv[:, :, 1], EPS, None, ALU.add).then_inc(ready, 1)

            def normalise(xn, x_, mv, rstd):
                for i in range(LT):
                    ins = nc.vector.tensor_scalar(xn[:, i, :], x_[:, i, :], mv[:, i, 0:1], rstd[:, i:i + 1],
                                                  ALU.subtract, ALU.mult)
                return ins

            def front_stats(b, half, par):
                dve.wait_ge(s_xf[par], 16 * (half + 1))
                variance(Steps(dve, v_ln1, LN1_STEPS, b), xf[par], st1, mv1, ve1, s_var1)

            def front_norm(b, half, par):
                dve.wait_ge(s_rstd1, b + 1)
                dve.wait_ge(s_mf[par], 16 * (half + 1))
                if not first(b):
                    dve.wait_ge(s_hs, b)
                normalise(xn1, xf[par], mv1, rs1).then_inc(s_xn1, 1)

            def front_pos(b, half, par):
                dve.wait_ge(s_posp, b + 1)
                nc.vector.tensor_tensor(pos[:, :], pf[0:Q, 0:G], posc[:, :], ALU.add).then_inc(s_pos, 1)
                nc.vector.tensor_tensor(fp[:, :, :].rearrange("p t a -> p (t a)"), pf[:, 128:128 + 2 * LT], fpc[:, :],
                                        ALU.add).then_inc(s_fpr, 1)
                dve.wait_ge(s_fpr, b + 1)
                st = Steps(dve, v_lin, LIN_STEPS, b)
                st.did(nc.vector.reciprocal(invf[:, :], fp[:, :, 0]))
                st.did(nc.vector.tensor_tensor(lp[:, :], lcol[:, :], fp[:, :, 1], ALU.add))
                st.wait()
                nc.vector.scalar_tensor_tensor(nlf[:, :], lp[:, :], -1.0, invf[:, :], ALU.mult, ALU.mult).then_inc(s_lin, 1)
                nc.vector.tensor_tensor(hclip[par][0:NX, :], pf[0:NX, 384:384 + C], own[:, :], ALU.mult).then_inc(s_hc, 1)

            def front_round(b):
                dve.wait_ge(a_ca, b + 1)
                nc.vector.tensor_scalar(cb_[:, :, :], ca_[:, :, :], -float(HALF), float(HALF), ALU.max,
                                        ALU.min).then_inc(v_cl, 1)
                dve.wait_ge(v_cl, b + 1)
                nc.vector.tensor_scalar(ca_[:, :, :], cb_[:, :, :], ROUND, ROUND, ALU.add, ALU.subtract).then_inc(s_rnd, 1)

            def front_kappa(b):
                if not first(b):
                    dve.wait_ge(s_prod, b)
                st = Steps(dve, v_kap, KAP_STEPS, b)
                for i in range(LT):
                    ins = nc.vector.tensor_scalar(posl[:, i, :], srow[:, :], fp[:, i, 0:1], lp[:, i:i + 1], ALU.mult, ALU.add)
                st.did(ins)
                st.wait()
                st.did(nc.vector.tensor_scalar(kl[:, :, :], posl[:, :, 0:LOW], 0.0, -1.0, ALU.min, ALU.max))
                st.did(nc.vector.tensor_scalar(kh[:, :, :], posl[:, :, S - HIGH:S], -float(L - 1), 0.0, ALU.add, ALU.max))
                st.wait()
                nc.vector.tensor_scalar(kh[:, :, :], kh[:, :, :], 1.0, None, ALU.min).then_inc(s_kap, 1)

            def front_scaled(b):
                dve.wait_ge(s_pos, b + 1)
                nc.vector.tensor_scalar(pos16[:, :], pos[:, :], MIDDLE, 0.5 / REACH, ALU.subtract, ALU.mult).then_inc(v_sel, 1)

            def front_dist(b):
                dve.wait_ge(v_sel, 2 * b + 1)
                nc.vector.tensor_tensor(
                    dist[:, :, :], pos16[:, :].rearrange("p (a g) -> p a g", a=1).to_broadcast([Q, NB, G]),
                    ctr[:, :].rearrange("p (j g) -> p j g", g=G), ALU.subtract).then_inc(v_sel, 1)

            def front_sel(b):
                dve.wait_ge(v_sel, 2 * b + 2)
                if not first(b):
                    dve.wait_ge(s_pp, NC * b)
                nc.vector.tensor_scalar(sel[:, 0:NB, :], dist[:, :, :], 0.0, None, ALU.is_equal).then_inc(s_sel, 1)

            def front_wm(b, k):
                if k == 0:
                    dve.wait_ge(s_rest, 2 * b + 2)
                    if not first(b):
                        dve.wait_ge(s_pp, NC * b)
                ins = nc.vector.tensor_scalar(wm[:, :, k * PH:(k + 1) * PH], wp[:, :, :], kmask[:, k:k + 1], None, ALU.mult)
                if k == NK - 1:
                    ins.then_inc(s_wm, 1)

            def front_clip(b):
                dve.wait_ge(s_prod, b + 1)
                if not first(b):
                    dve.wait_ge(s_clTp, b)
                nc.vector.tensor_reduce(clip[:, :, 0:H], pl[:, :, :].rearrange("p (t h) s -> p t h s", t=LT), AX.X, ALU.add)
                nc.vector.tensor_reduce(clip[:, :, H:NX], ph[:, :, :].rearrange("p (t h) s -> p t h s", t=LT), AX.X,
                                        ALU.add).then_inc(s_clip, 1)

            def mid_A(b, hp, m):
                if hp == 0 and m == 0:
                    dve.wait_ge(s_cT, b + 1)
                    if not first(b):
                        dve.wait_ge(s_attn, b)
                dve.wait_ge(s_pw, 8 * b + 2 * hp + m + 1)
                nc.vector.tensor_tensor(
                    A[:, m, 2 * hp:2 * hp + 2, :], pw[m][:, :].rearrange("p (h l) -> p h l", h=2),
                    cTm[:, m:m + 1, :].to_broadcast([P, 2, L]), ALU.mult).then_inc(s_A, 1)

            def back_stats(b, half, par):
                dve.wait_ge(s_x2, b + 1)
                hold()
                variance(Steps(dve, v_ln2, LN2_STEPS, b), x2[par], st2, mv2, ve2, s_var2)

            def back_norm(b, half, par):
                dve.wait_ge(s_rstd2, b + 1)
                if not first(b):
                    dve.wait_ge(s_h2, b)
                normalise(xn2, x2[par], mv2, rs2).then_inc(s_xn2, 1)

            def back_logits(b):
                dve.wait_ge(s_lgp, b + 1)
                nc.vector.tensor_tensor(
                    lg[:, :, :], pk[:, L:L + LT * E].rearrange("p (t e) -> p t e", e=E),
                    rb[:, :].rearrange("p (a e) -> p a e", a=1).to_broadcast([P, LT, E]), ALU.add).then_inc(s_lg, 1)

            def back_top(b):
                dve.wait_ge(s_lg, b + 1)
                hold()
                st = Steps(dve, v_top, TOP_STEPS, b)
                for i in range(LT):
                    ins = nc.vector.max(top[:, i, :], lg[:, i, :])
                st.did(ins)
                st.wait()
                hold()
                for i in range(LT):
                    ins = nc.vector.max_index(topi[:, i, :], top[:, i, :], lg[:, i, :])
                st.did(ins)
                st.wait()
                st.did(nc.vector.tensor_copy(topf[:, :, :], topi[:, :, :]))
                st.wait()
                for i in range(LT):
                    ins = nc.vector.tensor_scalar(top1[:, i, :], erow[:, :], topf[:, i, 0:1], None, ALU.is_equal)
                st.did(ins)
                st.wait()
                if not first(b):
                    dve.wait_ge(s_mTp, b)
                for i in range(LT):
                    ins = nc.vector.scalar_tensor_tensor(mask[:, i, :], erow[:, :], topf[:, i, 1:2], top1[:, i, :],
                                                         ALU.is_equal, ALU.add)
                ins.then_inc(s_mask, 1)

            def back_hm(b, n):
                dve.wait_ge(s_mb, 4 * b + n + 1)
                nc.vector.tensor_tensor(
                    hm[:, 2 * n:2 * n + 2, :], pk[:, :].rearrange("p (e l) -> p e l", e=2),
                    h2T[:, :].rearrange("p (a l) -> p a l", a=1).to_broadcast([P, 2, L]), ALU.mult).then_inc(s_hm, 1)

            def back_gate(b, half, par):
                dve.wait_ge(s_moe, b + 1)
                if not first(b):
                    dve.wait_ge(s_ob, b)
                nc.vector.tensor_tensor(moe[:, :, :], pz[:, 0:L].rearrange("p (t c) -> p t c", c=C),
                                        mk[par][:, 3:4, :].to_broadcast([P, LT, C]), ALU.mult).then_inc(s_gated, 1)

            def iteration(run, run_buf):
                run(-2, back_hm, 0)
                run_buf(2, front_stats)
                run(-2, back_hm, 1)
                run_buf(2, front_norm)
                run(0, front_clip)
                run(-2, back_hm, 2)
                run_buf(1, front_pos)
                run(-2, back_hm, 3)
                run(1, front_scaled)
                run(1, front_kappa)
                run(1, front_dist)
                run(1, front_round)
                run_buf(-1, back_stats)
                run(1, front_sel)
                run_buf(-1, back_norm)
                run(0, mid_A, 0, 0)
                run(0, mid_A, 0, 1)
                run(0, mid_A, 1, 0)
                run(0, mid_A, 1, 1)
                run(0, mid_A, 2, 0)
                run(0, mid_A, 2, 1)
                run(-1, back_logits)
                run(0, mid_A, 3, 0)
                run(0, mid_A, 3, 1)
                run(-1, back_top)
                run(1, front_wm, 0)
                run(1, front_wm, 1)
                run(1, front_wm, 2)
                run_buf(-2, back_gate)

            prologue()
            schedule(dve, iteration, -2, 2, 7, 17)

        @block.tensor
        def _(pe):
            mm = nc.tensor.matmul

            def prologue():
                pe.wait_ge(s_silc, 1)
                mm(pw[0][0:B, :], scT[:, :], wmod[:, 0:512], start=True, stop=True)
                mm(pw[1][0:B, 0:256], scT[:, :], wmod[:, 512:768], start=True, stop=True).then_inc(s_modp, 1)
                pe.wait_ge(s_biases, 16 * 3)
                pe.wait_ge(s_const, 16 * N_CONST)
                pe.wait_ge(s_zero, N_ZERO)
                pe.wait_ge(v_cast, 16)
                pe.wait_ge(s_cast, 2)
                pe.wait_ge(s_modc, 2)

            def mid_select(b, n):
                g0, g1 = CHUNKS[n]
                if n == 0:
                    pe.wait_ge(s_sel2, 2 * b + 2)
                    pe.wait_ge(s_wm, b + 1)
                if n >= 2 or not first(b):
                    pe.wait_ge(s_pick, NC * b + max(n - 1, 0))
                for g in range(g0, g1):
                    ins = mm(pp[n % 2][0:SLOT + NB, (g - g0) * NK * PH:(g - g0 + 1) * NK * PH], sel[:, :, g],
                             wm[:, g, :], start=True, stop=True)
                ins.then_inc(s_pp, 1)

            def mid_expand(b, hp, m):
                n = 2 * hp + m
                if n == 0:
                    pe.wait_ge(s_pick, NC * b + NC)
                if n >= 2 or not first(b):
                    pe.wait_ge(s_A, 8 * b + n - 1)
                for step in range(2):
                    x0 = step * H + 2 * hp
                    ins = mm(pw[m][:, :], expand[:, m * P:(m + 1) * P], pick[:, x0:x0 + 2, 0:L],
                             start=(step == 0), stop=(step == 1))
                ins.then_inc(s_pw, 1)

            def mid_attend(b, half, par, m):
                if m == 0:
                    pe.wait_ge(s_clT, b + 1)
                    pe.wait_ge(s_hc, b + 1)
                    pe.wait_ge(s_hs, b + 1)
                pe.wait_ge(s_A, 8 * b + 7 + m)
                for a in range(2):
                    for j in range(H // 2):
                        hh = 2 * j + a
                        mm(pa[32 * j:32 * j + 32, 0:L], hs[par][:, m * H + hh, :], A[:, m, hh, :],
                           start=(m == 0 and a == 0), stop=False)
                if m == LT - 1:
                    for j in range(H // 2):
                        ins = mm(pa[32 * j:32 * j + 32, 0:L], hclip[par][:, 32 * j:32 * j + 32], clipT[par][:, :],
                                 start=False, stop=True)
                    ins.then_inc(s_attn, 1)

            def front_hT(b):
                pe.wait_ge(s_h, b + 1)
                if not first(b):
                    pe.wait_ge(s_cT, b)
                for i in range(LT):
                    ins = nc.tensor.transpose(pf[:, i * P:(i + 1) * P], h[:, i, :], ident[:, :])
                ins.then_inc(s_hTp, 1)

            def front_wave(b):
                pe.wait_ge(s_hT, b + 1)
                mm(pf[0:40, L:2 * L], wvT[:, :], hT[:, 0:L], start=True, stop=True).then_inc(s_wvp, 1)

            def front_pos(b):
                pe.wait_ge(s_ft, b + 1)
                for k in range(NK):
                    mm(pf[0:Q, 0:G], spread[:, k, :], ft[:, k * G:(k + 1) * G], start=(k == 0), stop=(k == NK - 1))
                for i in range(LT):
                    mm(pf[:, 128 + 2 * i:130 + 2 * i], ft[:, i * P:(i + 1) * P], mean[:, :], start=True, stop=True)
                for i in range(LT):
                    ins = mm(pf[0:NX, 384:384 + C], ends[:, i, :], h[:, i, :],
                             start=(i == 0), stop=(i == LT - 1))
                ins.then_inc(s_posp, 1)

            def front_project(b, step):
                if step == 1:
                    pe.wait_ge(s_wT, NG * b + 2)
                else:
                    pe.wait_ge(s_hT, b + 1)
                    if not first(b):
                        pe.wait_ge(s_wT, NG * b)
                    if not first(b, MOE_LAG + 1):
                        pe.wait_ge(s_gated, b - MOE_LAG)
                for j in ((0, 1), (2,))[step]:
                    n = heads(j) * S
                    ins = mm(pz[0:n, j % 2 * L:(j % 2 + 1) * L], kwl[:, HG * S * j:HG * S * j + n], hT[:, 0:L],
                             start=True, stop=True)
                ins.then_inc(s_zp, 1)

            def front_rows(b, i):
                pe.wait_ge(s_hT, b + 1)
                if i == 0:
                    pe.wait_ge(s_hc, b + 1)
                    pe.wait_ge(s_fpr, b + 1)
                elif not first(b):
                    pe.wait_ge(s_aoT, b)
                dst = (pf, pa)[i][:, 0:NW]
                mm(dst, hT[:, i * P:(i + 1) * P], kwl[:, :], start=True, stop=False)
                mm(dst, one[:, :], kbp[:, :], start=False, stop=True).then_inc(s_wlp, 1)

            def front_clT(b):
                pe.wait_ge(s_clip, b + 1)
                pe.wait_ge(s_wl, 2 * b + 2)
                for i in range(LT):
                    ins = nc.tensor.transpose(pa[0:NX, i * P:(i + 1) * P], clip[:, i, :], ident[:, :])
                ins.then_inc(s_clTp, 1)

            def front_cT(b):
                pe.wait_ge(s_c, b + 1)
                pe.wait_ge(s_wl, 2 * b + 1)
                for m in range(LT):
                    for i in range(LT):
                        ins = nc.tensor.transpose(pf[:, m * L + i * P:m * L + (i + 1) * P],
                                                  cc_[:, i, m * P:(m + 1) * P], ident[:, :])
                ins.then_inc(s_cTp, 1)

            def back_y(b):
                pe.wait_ge(s_aoT, b + 1)
                if not first(b):
                    pe.wait_ge(s_hm, 4 * b)
                for i in range(LT):
                    ins = mm(pk[:, L + i * C:L + (i + 1) * C], aoT[:, i * P:(i + 1) * P], owT[:, :], start=True, stop=True)
                ins.then_inc(s_yp, 1)

            def back_h2T(b):
                pe.wait_ge(s_h2, b + 1)
                for i in range(LT):
                    ins = nc.tensor.transpose(pk[:, i * P:(i + 1) * P], h2[:, i, :], ident[:, :])
                ins.then_inc(s_h2Tp, 1)

            def back_router(b):
                pe.wait_ge(s_h2T, b + 1)
                for i in range(LT):
                    ins = mm(pk[:, L + i * E:L + (i + 1) * E], h2T[:, i * P:(i + 1) * P], rwT[:, :], start=True, stop=True)
                ins.then_inc(s_lgp, 1)

            def back_mT(b):
                pe.wait_ge(s_mask, b + 1)
                for i in range(LT):
                    ins = nc.tensor.transpose(pk[0:NE, i * P:(i + 1) * P], mask[:, i, :], ident[:, :])
                ins.then_inc(s_mTp, 1)

            def back_mb(b, n):
                if n == 0:
                    pe.wait_ge(s_mT, b + 1)
                    pe.wait_ge(s_lg, b + 1)
                else:
                    pe.wait_ge(s_hm, 4 * b + n)
                for j in range(2):
                    e = 2 * n + j
                    ins = mm(pk[:, j * L:(j + 1) * L], esel[:, e * P:(e + 1) * P], mkT[0:E, :], start=True, stop=True)
                ins.then_inc(s_mb, 1)

            def back_experts(b, i):
                if i == 0:
                    pe.wait_ge(s_hm, 4 * b + 4)
                    pe.wait_ge(s_wT, NG * (min(b + MOE_LAG, B - 1) + 1 if isinstance(b, int) else b + MOE_LAG + 1))
                dst = pz[:, i * C:(i + 1) * C]
                for e in range(E):
                    mm(dst, hm[:, e, i * P:(i + 1) * P], weT[:, e, :], start=(e == 0), stop=False)
                ins = mm(dst, mkT[:, i * P:(i + 1) * P], ebp[:, :], start=False, stop=True)
                if i == LT - 1:
                    ins.then_inc(s_moe, 1)

            def iteration(run, run_buf):
                run(0, mid_expand, 0, 0)
                run(0, mid_expand, 0, 1)
                run(1, front_rows, 0)
                run(0, mid_expand, 1, 0)
                run(0, mid_expand, 1, 1)
                run(-1, back_h2T)
                run(0, mid_expand, 2, 0)
                run(0, mid_expand, 2, 1)
                run(-1, back_router)
                run(0, mid_expand, 3, 0)
                run(0, mid_expand, 3, 1)
                run_buf(0, mid_attend, 0)
                run_buf(0, mid_attend, 1)
                run(-1, back_mT)
                run(1, front_cT)
                run(1, front_rows, 1)
                run(-1, back_mb, 0)
                run(2, front_hT)
                run(1, mid_select, 0)
                run(1, mid_select, 1)
                run(2, front_wave)
                run(-1, back_mb, 1)
                run(1, mid_select, 2)
                run(2, front_project, 0)
                run(1, mid_select, 3)
                run(-1, back_mb, 2)
                run(1, mid_select, 4)
                run(2, front_pos)
                run(1, mid_select, 5)
                run(1, mid_select, 6)
                run(-1, back_mb, 3)
                run(2, front_project, 1)
                run(1, mid_select, 7)
                run(1, mid_select, 8)
                run(1, front_clT)
                run(0, back_y)
                run(1, mid_select, 9)
                run(1, mid_select, 10)
                run(-1, back_experts, 0)
                run(1, mid_select, 11)
                run(1, mid_select, 12)
                run(-1, back_experts, 1)

            prologue()
            schedule(pe, iteration, -2, 1, 7, 16)


def kernel(L0_attn_x, L0_attn_wave_w, L0_attn_wave_b, L0_attn_kernel_w, L0_attn_kernel_b, L0_attn_out_w,
           L0_ffn_router_w, L0_ffn_router_b, L0_ffn_expert_w, L0_ffn_expert_b, L0_c, L0_wmod):
    import concourse.bacc as bacc
    from concourse.bass_utils import run_bass_kernel_spmd

    a = lambda x: np.ascontiguousarray(np.asarray(x))
    K = L0_attn_kernel_w.shape[0] // H
    arrays = constants()
    arrays["x"] = a(L0_attn_x)
    arrays["kwl"] = a(np.asarray(L0_attn_kernel_w).reshape(H, K, C)[:, :S].transpose(2, 0, 1)).reshape(C, NW)
    kb = np.zeros(NG * HG * S, np.float32)
    kb[:NW] = np.asarray(L0_attn_kernel_b).reshape(H, K)[:, :S].reshape(NW)
    arrays["kb"] = kb.reshape(NG, HG * S).T
    arrays["kbl"] = a(np.asarray(L0_attn_kernel_b).reshape(H, K)[:, :S].reshape(1, NW))
    arrays["wvT"], arrays["wvb"] = np.zeros((C, 40), np.float32), np.zeros((40, 1), np.float32)
    for r0, r1 in ((0, 0), (32, H)):
        arrays["wvT"][:, r0:r0 + H] = np.asarray(L0_attn_wave_w)[r1:r1 + H].T
        arrays["wvb"][r0:r0 + H, 0] = np.asarray(L0_attn_wave_b)[r1:r1 + H]
    arrays["owT"] = a(np.asarray(L0_attn_out_w).T)
    arrays["rwT"] = a(np.asarray(L0_ffn_router_w).T)
    arrays["rb"] = a(L0_ffn_router_b)
    arrays["weT"] = a(np.asarray(L0_ffn_expert_w).transpose(2, 0, 1))
    arrays["eb"] = a(np.tile(np.asarray(L0_ffn_expert_b), (NP, 1)))
    arrays["cT"] = a(np.asarray(L0_c).T)
    arrays["wmod"] = a(L0_wmod)

    for pack, (rows, columns) in PACKS.items():
        arrays[pack] = np.concatenate([np.reshape(arrays.pop(n), (rows, width)) for n, width in columns], axis=1)

    nc = bacc.Bacc("TRN2", target_bir_lowering=False, num_devices=1)
    t, feed = {}, {}
    for name, v in arrays.items():
        v = a(v)
        feed[f"in_{name}"] = v
        t[name] = nc.dram_tensor(f"in_{name}", v.shape, mybir.dt.from_np(v.dtype), kind="ExternalInput").ap()
    t["mod"] = nc.dram_tensor("mod_rows", (B, 6, C), F32, kind="Internal").ap()
    t["weights"] = nc.dram_tensor("weights", (NW, L), F32, kind="Internal").ap()
    t["out"] = nc.dram_tensor("out_0", (B, L, C), F32, kind="ExternalOutput").ap()
    build(nc, t)
    r = run_bass_kernel_spmd(nc, [feed], core_ids=[0])
    return r.results[0]["out_0"]
```
